# Optimizing a Trainium2 kernel written in Bass

```python
import numpy as np
import jax
import jax.numpy as jnp

def _softmax(x, axis=-1):
    return jax.nn.softmax(x, axis=axis)

def _gelu(x):
    return jax.nn.gelu(x, approximate=True)

def _silu(x):
    return jax.nn.silu(x)

def _sigmoid(x):
    return jax.nn.sigmoid(x)

def _layernorm(x, axis=-1, eps=1e-05):
    m = jnp.mean(x, axis=axis, keepdims=True)
    v = jnp.var(x, axis=axis, keepdims=True)
    return (x - m) / jnp.sqrt(v + eps)

def _scatter_add(tgt, idx, src, axis=0):
    return tgt.at[idx].add(src)

def _segment_sum(src, seg, n):
    return jax.ops.segment_sum(src, seg, n)
kernel_name = 'mk_recurrent_d1_jaxref_r4_d04828'

def setup_inputs(seed: int=0):
    np.random.seed(seed)
    _w = jnp.asarray

    def _L0_attn_setup():
        import jax, jax.numpy as jnp
        import numpy as np
        NHEAD = 16

        def _forward(x, time_maa_x, time_maa, time_maa_w1, time_maa_w2, time_decay, time_decay_w1, time_decay_w2, time_aaaaa, time_aaa_w1, time_aaa_w2, time_kkk_w1, time_kkk_w2, gate_w1, gate_w2, time_misc_a, ma_w1, ma_w2, time_misc_k, mk_w1, mk_w2, receptance, key_w, value, output, ln_w, ln_b, time_faaaa):
            B, T, C = x.shape
            H, N = (NHEAD, C // NHEAD)
            xprev = jnp.pad(x, ((0, 0), (1, 0), (0, 0)))[:, :T]
            xx = xprev - x
            xxx = x + xx * time_maa_x
            mix = jnp.tanh(xxx @ time_maa_w1.T).reshape(B, T, 4, -1)
            deltas = jnp.einsum('btfd,fcd->fbtc', mix, time_maa_w2)
            xrg, xwa, xk, xv = x[None] + xx[None] * (time_maa + deltas)
            r = xrg @ receptance.T
            g = jnp.tanh(xrg @ gate_w1.T) @ gate_w2.T
            k = xk @ key_w.T
            kk1 = jnp.tanh(xk @ time_kkk_w1.T)
            mk1 = xk @ mk_w1.T
            v = xv @ value.T
            w1 = jnp.tanh(xwa @ time_decay_w1.T)
            a1 = xwa @ time_aaa_w1.T
            ma1 = xwa @ ma_w1.T
            w = -jax.nn.softplus(-(time_decay + w1 @ time_decay_w2.T)) - 0.5
            kk = k + kk1 @ time_kkk_w2.T
            kk = kk.reshape(B, T, H, N)
            kk = kk / jnp.maximum(jnp.linalg.norm(kk, axis=-1, keepdims=True), 1e-12)
            kk = kk.reshape(B, T, C)
            a = jax.nn.sigmoid(time_aaaaa + a1 @ time_aaa_w2.T)
            ma = jax.nn.sigmoid(time_misc_a + ma1 @ ma_w2.T)
            k = k * ma + k * a * (1 - ma)
            mk = jax.nn.sigmoid(time_misc_k + mk1 @ mk_w2.T)
            k = k * jnp.exp(w * mk)
            b = -kk * a

            def heads(z):
                return z.reshape(B, T, H, N).transpose(1, 0, 2, 3)
            rh, wh, kh, vh, kkh, bh = map(heads, (r, w, k, v, kk, b))

            def step(S, inp):
                r_, w_, k_, v_, kk_, b_ = inp
                sab = jnp.einsum('bhvk,bhk->bhv', S, kk_)
                S = S * jnp.exp(w_)[:, :, None, :] + sab[..., None] * b_[:, :, None, :] + v_[..., None] * k_[:, :, None, :]
                y = jnp.einsum('bhvk,bhk->bhv', S, r_)
                return (S, y)
            S0 = jnp.zeros((B, H, N, N), x.dtype)
            _, y = jax.lax.scan(step, S0, (rh, wh, kh, vh, kkh, bh))
            y = y.transpose(1, 0, 2, 3)
            mu = y.mean(-1, keepdims=True)
            var = ((y - mu) ** 2).mean(-1, keepdims=True)
            yn = (y - mu) / jnp.sqrt(var + 0.00064) * ln_w.reshape(H, N) + ln_b.reshape(H, N)
            r4 = r.reshape(B, T, H, N)
            k4 = k.reshape(B, T, H, N)
            v4 = v.reshape(B, T, H, N)
            bonus = (r4 * k4 * time_faaaa.reshape(H, N)).sum(-1, keepdims=True) * v4
            out = (yn + bonus).reshape(B, T, C) * g
            return out @ output.T
        key = jax.random.key(seed)
        ks = iter(jax.random.split(key, 40))
        B, T, C = (2, 256, 256)

        def n(shape, s=1.0):
            return jax.random.normal(next(ks), shape, jnp.float32) * s

        def u(shape, lo, hi):
            return jax.random.uniform(next(ks), shape, jnp.float32, lo, hi)
        d = {}
        d['x'] = n((B, T, C))
        d['time_maa_x'] = u((1, 1, C), 0.0, 1.0)
        d['time_maa'] = u((4, 1, 1, C), 0.0, 1.0)
        d['time_maa_w1'] = n((128, C), 0.02)
        d['time_maa_w2'] = n((4, C, 32), 0.05)
        d['time_decay'] = u((1, 1, C), -6.5, -1.5)
        d['time_decay_w1'] = n((64, C), 0.02)
        d['time_decay_w2'] = n((C, 64), 0.05)
        d['time_aaaaa'] = n((1, 1, C), 0.1)
        d['time_aaa_w1'] = n((16, C), 0.02)
        d['time_aaa_w2'] = n((C, 16), 0.05)
        d['time_kkk_w1'] = n((16, C), 0.02)
        d['time_kkk_w2'] = n((C, 16), 0.05)
        d['gate_w1'] = n((128, C), 0.05)
        d['gate_w2'] = n((C, 128), 0.05)
        d['time_misc_a'] = n((1, 1, C), 0.1)
        d['ma_w1'] = n((16, C), 0.02)
        d['ma_w2'] = n((C, 16), 0.05)
        d['time_misc_k'] = n((1, 1, C), 0.1)
        d['mk_w1'] = n((16, C), 0.02)
        d['mk_w2'] = n((C, 16), 0.05)
        s = 0.5 / C ** 0.5
        d['receptance'] = u((C, C), -s, s)
        d['key_w'] = u((C, C), -0.1 * s, 0.1 * s)
        d['value'] = u((C, C), -s, s)
        d['output'] = n((C, C), 0.02)
        d['ln_w'] = jnp.ones((C,), jnp.float32)
        d['ln_b'] = jnp.zeros((C,), jnp.float32)
        d['time_faaaa'] = n((C,), 0.1)
        return d
    _L0_attn_in = _L0_attn_setup()

    def _L0_ffn_setup():
        import jax, jax.numpy as jnp
        import numpy as np
        D_IN = 256
        D_OUT = 256
        D_QUERY = 64
        N_HEADS = 8
        N_EXPERTS = 16384
        N_SQRT = 64
        TOPK = 10
        DQ_HALF = D_QUERY // 2
        key = jax.random.key(seed)
        ks = jax.random.split(key, 7)
        B, S = (2, 256)
        x = jax.random.normal(ks[0], (B, S, D_IN), dtype=jnp.float32)
        Wq = jax.random.normal(ks[1], (D_IN, D_QUERY * N_HEADS), dtype=jnp.float32) / np.sqrt(D_IN)
        bq = jnp.zeros((D_QUERY * N_HEADS,), dtype=jnp.float32)
        K1 = jax.random.normal(ks[2], (N_SQRT, DQ_HALF), dtype=jnp.float32)
        K2 = jax.random.normal(ks[3], (N_SQRT, DQ_HALF), dtype=jnp.float32)
        W_up = jax.random.normal(ks[4], (N_EXPERTS, D_OUT), dtype=jnp.float32)
        W_down = jax.random.normal(ks[5], (N_EXPERTS, D_IN), dtype=jnp.float32)
        return {'x': x, 'Wq': Wq, 'bq': bq, 'K1': K1, 'K2': K2, 'W_up': W_up, 'W_down': W_down}
    _L0_ffn_in = _L0_ffn_setup()
    _d = {'L0_attn_x': _L0_attn_in['x'], 'L0_attn_time_maa_x': _L0_attn_in['time_maa_x'], 'L0_attn_time_maa': _L0_attn_in['time_maa'], 'L0_attn_time_maa_w1': _L0_attn_in['time_maa_w1'], 'L0_attn_time_maa_w2': _L0_attn_in['time_maa_w2'], 'L0_attn_time_decay': _L0_attn_in['time_decay'], 'L0_attn_time_decay_w1': _L0_attn_in['time_decay_w1'], 'L0_attn_time_decay_w2': _L0_attn_in['time_decay_w2'], 'L0_attn_time_aaaaa': _L0_attn_in['time_aaaaa'], 'L0_attn_time_aaa_w1': _L0_attn_in['time_aaa_w1'], 'L0_attn_time_aaa_w2': _L0_attn_in['time_aaa_w2'], 'L0_attn_time_kkk_w1': _L0_attn_in['time_kkk_w1'], 'L0_attn_time_kkk_w2': _L0_attn_in['time_kkk_w2'], 'L0_attn_gate_w1': _L0_attn_in['gate_w1'], 'L0_attn_gate_w2': _L0_attn_in['gate_w2'], 'L0_attn_time_misc_a': _L0_attn_in['time_misc_a'], 'L0_attn_ma_w1': _L0_attn_in['ma_w1'], 'L0_attn_ma_w2': _L0_attn_in['ma_w2'], 'L0_attn_time_misc_k': _L0_attn_in['time_misc_k'], 'L0_attn_mk_w1': _L0_attn_in['mk_w1'], 'L0_attn_mk_w2': _L0_attn_in['mk_w2'], 'L0_attn_receptance': _L0_attn_in['receptance'], 'L0_attn_key_w': _L0_attn_in['key_w'], 'L0_attn_value': _L0_attn_in['value'], 'L0_attn_output': _L0_attn_in['output'], 'L0_attn_ln_w': _L0_attn_in['ln_w'], 'L0_attn_ln_b': _L0_attn_in['ln_b'], 'L0_attn_time_faaaa': _L0_attn_in['time_faaaa'], 'L0_ffn_Wq': _L0_ffn_in['Wq'], 'L0_ffn_bq': _L0_ffn_in['bq'], 'L0_ffn_K1': _L0_ffn_in['K1'], 'L0_ffn_K2': _L0_ffn_in['K2'], 'L0_ffn_W_up': _L0_ffn_in['W_up'], 'L0_ffn_W_down': _L0_ffn_in['W_down']}
    _x0 = _d['L0_attn_x']
    _d['L0_attn_x'] = jax.random.normal(jax.random.fold_in(jax.random.key(seed), 1), (4, 2048, 256), dtype=_x0.dtype)
    del _x0
    return _d

def reference(L0_attn_x, L0_attn_time_maa_x, L0_attn_time_maa, L0_attn_time_maa_w1, L0_attn_time_maa_w2, L0_attn_time_decay, L0_attn_time_decay_w1, L0_attn_time_decay_w2, L0_attn_time_aaaaa, L0_attn_time_aaa_w1, L0_attn_time_aaa_w2, L0_attn_time_kkk_w1, L0_attn_time_kkk_w2, L0_attn_gate_w1, L0_attn_gate_w2, L0_attn_time_misc_a, L0_attn_ma_w1, L0_attn_ma_w2, L0_attn_time_misc_k, L0_attn_mk_w1, L0_attn_mk_w2, L0_attn_receptance, L0_attn_key_w, L0_attn_value, L0_attn_output, L0_attn_ln_w, L0_attn_ln_b, L0_attn_time_faaaa, L0_ffn_Wq, L0_ffn_bq, L0_ffn_K1, L0_ffn_K2, L0_ffn_W_up, L0_ffn_W_down):

    def _L0_attn_ref(x, time_maa_x, time_maa, time_maa_w1, time_maa_w2, time_decay, time_decay_w1, time_decay_w2, time_aaaaa, time_aaa_w1, time_aaa_w2, time_kkk_w1, time_kkk_w2, gate_w1, gate_w2, time_misc_a, ma_w1, ma_w2, time_misc_k, mk_w1, mk_w2, receptance, key_w, value, output, ln_w, ln_b, time_faaaa):
        import jax, jax.numpy as jnp
        import numpy as np
        NHEAD = 16

        def _forward(x, time_maa_x, time_maa, time_maa_w1, time_maa_w2, time_decay, time_decay_w1, time_decay_w2, time_aaaaa, time_aaa_w1, time_aaa_w2, time_kkk_w1, time_kkk_w2, gate_w1, gate_w2, time_misc_a, ma_w1, ma_w2, time_misc_k, mk_w1, mk_w2, receptance, key_w, value, output, ln_w, ln_b, time_faaaa):
            B, T, C = x.shape
            H, N = (NHEAD, C // NHEAD)
            xprev = jnp.pad(x, ((0, 0), (1, 0), (0, 0)))[:, :T]
            xx = xprev - x
            xxx = x + xx * time_maa_x
            mix = jnp.tanh(xxx @ time_maa_w1.T).reshape(B, T, 4, -1)
            deltas = jnp.einsum('btfd,fcd->fbtc', mix, time_maa_w2)
            xrg, xwa, xk, xv = x[None] + xx[None] * (time_maa + deltas)
            r = xrg @ receptance.T
            g = jnp.tanh(xrg @ gate_w1.T) @ gate_w2.T
            k = xk @ key_w.T
            kk1 = jnp.tanh(xk @ time_kkk_w1.T)
            mk1 = xk @ mk_w1.T
            v = xv @ value.T
            w1 = jnp.tanh(xwa @ time_decay_w1.T)
            a1 = xwa @ time_aaa_w1.T
            ma1 = xwa @ ma_w1.T
            w = -jax.nn.softplus(-(time_decay + w1 @ time_decay_w2.T)) - 0.5
            kk = k + kk1 @ time_kkk_w2.T
            kk = kk.reshape(B, T, H, N)
            kk = kk / jnp.maximum(jnp.linalg.norm(kk, axis=-1, keepdims=True), 1e-12)
            kk = kk.reshape(B, T, C)
            a = jax.nn.sigmoid(time_aaaaa + a1 @ time_aaa_w2.T)
            ma = jax.nn.sigmoid(time_misc_a + ma1 @ ma_w2.T)
            k = k * ma + k * a * (1 - ma)
            mk = jax.nn.sigmoid(time_misc_k + mk1 @ mk_w2.T)
            k = k * jnp.exp(w * mk)
            b = -kk * a

            def heads(z):
                return z.reshape(B, T, H, N).transpose(1, 0, 2, 3)
            rh, wh, kh, vh, kkh, bh = map(heads, (r, w, k, v, kk, b))

            def step(S, inp):
                r_, w_, k_, v_, kk_, b_ = inp
                sab = jnp.einsum('bhvk,bhk->bhv', S, kk_)
                S = S * jnp.exp(w_)[:, :, None, :] + sab[..., None] * b_[:, :, None, :] + v_[..., None] * k_[:, :, None, :]
                y = jnp.einsum('bhvk,bhk->bhv', S, r_)
                return (S, y)
            S0 = jnp.zeros((B, H, N, N), x.dtype)
            _, y = jax.lax.scan(step, S0, (rh, wh, kh, vh, kkh, bh))
            y = y.transpose(1, 0, 2, 3)
            mu = y.mean(-1, keepdims=True)
            var = ((y - mu) ** 2).mean(-1, keepdims=True)
            yn = (y - mu) / jnp.sqrt(var + 0.00064) * ln_w.reshape(H, N) + ln_b.reshape(H, N)
            r4 = r.reshape(B, T, H, N)
            k4 = k.reshape(B, T, H, N)
            v4 = v.reshape(B, T, H, N)
            bonus = (r4 * k4 * time_faaaa.reshape(H, N)).sum(-1, keepdims=True) * v4
            out = (yn + bonus).reshape(B, T, C) * g
            return out @ output.T
        return _forward(x, time_maa_x, time_maa, time_maa_w1, time_maa_w2, time_decay, time_decay_w1, time_decay_w2, time_aaaaa, time_aaa_w1, time_aaa_w2, time_kkk_w1, time_kkk_w2, gate_w1, gate_w2, time_misc_a, ma_w1, ma_w2, time_misc_k, mk_w1, mk_w2, receptance, key_w, value, output, ln_w, ln_b, time_faaaa)

    def _L0_ffn_ref(x, Wq, bq, K1, K2, W_up, W_down):
        import jax, jax.numpy as jnp
        import numpy as np
        D_IN = 256
        D_OUT = 256
        D_QUERY = 64
        N_HEADS = 8
        N_EXPERTS = 16384
        N_SQRT = 64
        TOPK = 10
        DQ_HALF = D_QUERY // 2
        B, S, _ = x.shape
        q = (x @ Wq + bq).reshape(B, S, N_HEADS, D_QUERY)
        q1, q2 = (q[..., :DQ_HALF], q[..., DQ_HALF:])
        s1 = jnp.einsum('bshd,nd->bshn', q1, K1)
        s2 = jnp.einsum('bshd,nd->bshn', q2, K2)
        v1, i1 = jax.lax.top_k(s1, TOPK)
        v2, i2 = jax.lax.top_k(s2, TOPK)
        all_scores = (v1[..., :, None] + v2[..., None, :]).reshape(B, S, N_HEADS, TOPK * TOPK)
        all_indices = (i1[..., :, None] * N_SQRT + i2[..., None, :]).reshape(B, S, N_HEADS, TOPK * TOPK)
        vals, best = jax.lax.top_k(all_scores, TOPK)
        expert_idx = jnp.take_along_axis(all_indices, best, axis=-1)
        w_down = W_down[expert_idx]
        w_up = W_up[expert_idx]
        scores = jax.nn.softmax(vals, axis=-1)
        h = jnp.einsum('bsd,bshkd->bshk', x, w_down)
        h = jax.nn.gelu(h, approximate=False) * scores
        out = jnp.einsum('bshk,bshkd->bsd', h, w_up)
        return out
    x = L0_attn_x
    xn = _layernorm(x, axis=-1)
    s = _L0_attn_ref(xn, L0_attn_time_maa_x, L0_attn_time_maa, L0_attn_time_maa_w1, L0_attn_time_maa_w2, L0_attn_time_decay, L0_attn_time_decay_w1, L0_attn_time_decay_w2, L0_attn_time_aaaaa, L0_attn_time_aaa_w1, L0_attn_time_aaa_w2, L0_attn_time_kkk_w1, L0_attn_time_kkk_w2, L0_attn_gate_w1, L0_attn_gate_w2, L0_attn_time_misc_a, L0_attn_ma_w1, L0_attn_ma_w2, L0_attn_time_misc_k, L0_attn_mk_w1, L0_attn_mk_w2, L0_attn_receptance, L0_attn_key_w, L0_attn_value, L0_attn_output, L0_attn_ln_w, L0_attn_ln_b, L0_attn_time_faaaa)
    g = _silu(_L0_ffn_ref(xn, L0_ffn_Wq, L0_ffn_bq, L0_ffn_K1, L0_ffn_K2, L0_ffn_W_up, L0_ffn_W_down))
    x = x + s * g
    return x

_drawn_inputs = setup_inputs


def setup_inputs(seed=0):
    import zlib

    import numpy as np

    out = dict(_drawn_inputs(seed))
    spreads = {'L0_attn_ln_w': (1.0, 0.6), 'L0_attn_ln_b': (0.0, 0.1), 'L0_ffn_bq': (0.0, 0.1)}
    factors = {'L0_attn_time_maa_x': 6.044,
     'L0_attn_time_maa_w1': 3.064,
     'L0_attn_time_maa_w2': 3.073,
     'L0_attn_time_decay': 3.032,
     'L0_attn_time_decay_w1': 8.0,
     'L0_attn_time_decay_w2': 8.0,
     'L0_attn_time_aaaaa': 8.0,
     'L0_attn_time_aaa_w1': 8.0,
     'L0_attn_time_aaa_w2': 8.0,
     'L0_attn_time_kkk_w1': 8.0,
     'L0_attn_time_kkk_w2': 8.0,
     'L0_attn_time_misc_a': 8.0,
     'L0_attn_ma_w1': 8.0,
     'L0_attn_ma_w2': 8.0,
     'L0_attn_time_misc_k': 8.0,
     'L0_attn_mk_w1': 8.0,
     'L0_attn_mk_w2': 8.0,
     'L0_attn_time_faaaa': 43.933}
    for name, (base, spread) in spreads.items():
        noise = np.random.default_rng([zlib.crc32(name.encode()), seed]).standard_normal(out[name].shape)
        drawn = base * np.exp(spread * noise) if base else spread * noise
        out[name] = jnp.asarray(drawn.astype(out[name].dtype))
    for name, factor in factors.items():
        out[name] = (out[name] * factor).astype(out[name].dtype)
    return out
```

```python
from contextlib import ExitStack

import concourse.bass as bass
from concourse import mybir

P = 128
B = 4
C = 256
HALVES = 2
J = 32
TOK = B * J
H = 16
N = 16
HH = 8
FH = 8
NKEY = 64
TOPK = 10
PAIRS = [(0, 10), (1, 5), (2, 3), (3, 2), (4, 2), (5, 1), (6, 1), (7, 1), (8, 1), (9, 1)]
NCAND = sum(n for _, n in PAIRS)
SEL = FH * TOPK
ER = 32
CH = 16
NCH = TOK // CH
DVE_LINKS = 174
WSCALE = 8192.0
NEG = -3.0e38
LN_EPS = 1e-5
GN_EPS = 0.00064

F32 = mybir.dt.float32
F16 = mybir.dt.float16
U32 = mybir.dt.uint32
I32 = mybir.dt.int32
ALU = mybir.AluOpType
ACT = mybir.ActivationFunctionType
AX = mybir.AxisListType.X

LAYOUT = [
    ("w1", 2 * 128), ("w2", 4 * 256), ("wr", 2 * 256), ("wk", 2 * 256), ("wv", 2 * 256), ("gw1", 2 * 128),
    ("lowa", 2 * 96), ("lowk", 2 * 48), ("dec2", 256), ("aaa2", 256), ("ma2", 256), ("kkk2", 256), ("mk2", 256),
    ("gw2", 256), ("wq", 2 * 512), ("kbd", 256), ("wo", 2 * 256), ("ident", 128), ("headones", 128),
    ("headcol", 8), ("headrow", 2 * 128), ("maax", 2), ("maa", 8), ("td", 2), ("ba", 2), ("bma", 2), ("bmk", 2),
    ("fa", 2), ("bq", 4), ("lnw", 256), ("lnb", 256), ("iota_e", 256), ("iota_c", NCAND + 1), ("mhalf", 16),
]
COL = {}
_at = 0
for _n, _w in LAYOUT:
    COL[_n] = _at
    _at += _w
NCONST = _at


class Part:

    def __init__(self, tensor, at, width):
        self.tensor, self.at, self.width = tensor, at, width

    def __getitem__(self, key):
        return self.tensor[:, self.at:self.at + self.width]


def v(t, off, *dims, p0=0, n=P):
    if isinstance(t, Part):
        off, t = off + t.at, t.tensor
    a = t[p0:p0 + n, :]
    return bass.AP(a.tensor, a.offset + off, [list(a.ap[0])] + [list(d) for d in dims])


def build(nc, x, params, down, up, vscratch, out, tiles):
    with ExitStack() as ctx:
        def sb(name, width, dt=F32, parts=P):
            return ctx.enter_context(nc.sbuf_tensor(name, [parts, width], dt))

        def sem(name):
            return ctx.enter_context(nc.semaphore(name))

        def bank(name):
            return ctx.enter_context(nc.psum_tensor(name, [P, 512], F32))

        ps_u = bank("ps_u")
        ps_a0, ps_a1 = bank("ps_a0"), bank("ps_a1")
        ps_h = [bank("ps_h0"), bank("ps_h1")]
        ps_s = [bank("ps_s0"), bank("ps_s1")]
        ps_f = bank("ps_f")

        cst = sb("cst", NCONST)
        wdown = sb("wdown", HALVES * ER * P)
        wup = sb("wup", ER * C)
        iota_e16 = sb("iota_e16", 256, F16)
        ntd = sb("ntd", 2)
        hba = sb("hba", 2)
        hbma = sb("hbma", 2)
        hbmk = sb("hbmk", 2)
        mhalf_b = sb("mhalf_b", 1)

        def c_(name, off, *dims, p0=0, n=P):
            return v(cst, COL[name] + off, *dims, p0=p0, n=n)

        SW = HALVES * B * N
        hist = sb("hist", J * SW)
        lent = [0]

        def early(width):
            at = lent[0]
            lent[0] += width
            assert lent[0] <= (J - 1) * SW
            return Part(hist, at, width)

        x_in = sb("x_in", C)
        stats = sb("stats", 6)
        meanvar = sb("meanvar", 2)
        vareps = sb("vareps", 1)
        rstd = sb("rstd", 1)
        xn = sb("xn", C)
        xt = sb("xt", HALVES * B * (J + 1))
        xnt = sb("xnt", HALVES * TOK)
        xx = early(HALVES * TOK)
        xxx = sb("xxx", HALVES * TOK)
        mix = early(TOK)
        xf = early(4 * HALVES * TOK)
        r_t = sb("r_t", HALVES * TOK)
        k_t = sb("k_t", HALVES * TOK)
        v_t = xn
        v_tok = sb("v_tok", C)
        g_tok = sb("g_tok", C)
        tgate = early(TOK)
        low_a = early(TOK)
        low_k = early(TOK)
        absz = sb("absz", HALVES * TOK)
        reluz = sb("reluz", HALVES * TOK)
        tanh_a = early(HALVES * TOK)
        tanh_ma = early(HALVES * TOK)
        tanh_mk = early(HALVES * TOK)
        kk_raw = sb("kk_raw", HALVES * TOK)
        kk_sq = xxx
        ss = sb("ss", H)
        inv_n = sb("inv_n", H)
        inv_nt = sb("inv_nt", TOK)
        a_t = sb("a_t", HALVES * TOK)
        kk = kk_raw
        b_t = sb("b_t", HALVES * TOK)
        spl = reluz
        expw = sb("expw", HALVES * TOK)
        wm = absz
        expwm = absz
        mk_t = tanh_mk
        kmul = sb("kmul", HALVES * TOK)
        k_fin = kmul
        rkf = xxx
        bv = sb("bv", C)
        q_t = early(4 * TOK)
        scores = sb("scores", FH * 2 * NKEY)
        scores2 = sb("scores2", 2 * NKEY)
        vk = sb("vk", HALVES * N * TOK)

        t_kk = sb("t_kk", SW)
        t_d = sb("t_d", SW)
        t_dvk = sb("t_dvk", SW)
        t_o = sb("t_o", SW)
        z = vk

        topv = sb("topv", 16 * 16)
        topi = sb("topi", 16 * 16, U32)
        topif = sb("topif", 16 * 16)
        hi_f = sb("hi_f", FH * 16)
        cand = sb("cand", FH * NCAND)
        candi = sb("candi", FH * NCAND)
        cand2 = sb("cand2", NCAND)
        vals = sb("vals", FH * 16)
        pos = sb("pos", FH * 16, U32)
        posf = sb("posf", FH * 16)
        eqp = sb("eqp", FH // 2 * TOPK * NCAND)
        sel = sb("sel", SEL)
        sel_i = sb("sel_i", SEL, I32)
        sel_lo = sb("sel_lo", SEL, I32)
        sel_hi = sb("sel_hi", SEL, I32)
        lof = sb("lof", SEL)
        hif = sb("hif", SEL)
        dif = sb("dif", SEL)
        ex = sb("ex", SEL)
        sume = sb("sume", FH)
        rsum = sb("rsum", FH)
        wsel = sb("wsel", SEL)
        hi_t = sb("hi_t", TOK, F16, SEL)
        lo_t = sb("lo_t", TOK, F16, SEL)
        w1_t = sb("w1_t", TOK, F16, SEL)
        w2_t = sb("w2_t", TOK, F16, SEL)
        oh_a = [sb(f"oh_a{i}", CH * P, F16, SEL) for i in range(2)]
        oh_e = [sb(f"oh_e{i}", CH * ER, F16, SEL) for i in range(2)]
        oh_1 = [sb(f"oh_1{i}", CH * ER, F16, SEL) for i in range(2)]
        oh_2 = [sb(f"oh_2{i}", CH * ER, F16, SEL) for i in range(2)]
        gh = sb("gh", ER * TOK)

        ysum = sb("ysum", H)
        ymean = sb("ymean", H)
        yc = sb("yc", C)
        ysq = sb("ysq", C)
        yvs = sb("yvs", H)
        yve = sb("yve", H)
        yrs = sb("yrs", H)
        yn = sb("yn", C)
        yn2 = sb("yn2", C)
        yt = sb("yt", HALVES * TOK)
        th_f = ysq
        sg_f = yc
        silu_f = yn2
        o_s = yn2
        y_out = sb("y_out", C)

        s_par = sem("s_par")
        s_pre = sem("s_pre")
        s_x = sem("s_x")
        s_xfree = sem("s_xfree")
        s_vare = sem("s_vare")
        s_rstd = sem("s_rstd")
        s_xn = sem("s_xn")
        s_xtp = sem("s_xtp")
        s_xt = sem("s_xt")
        s_xxx = sem("s_xxx")
        s_mixp = sem("s_mixp")
        s_mix = sem("s_mix")
        s_delta = sem("s_delta")
        s_xf = sem("s_xf")
        s_q = sem("s_q")
        s_qt = sem("s_qt")
        s_scp = sem("s_scp")
        s_scores = sem("s_scores")
        s_p1 = sem("s_p1")
        s_c1 = sem("s_c1")
        s_p2 = sem("s_p2")
        s_vt = sem("s_vt")
        s_c2 = sem("s_c2")
        s_p3 = sem("s_p3")
        s_c3 = sem("s_c3")
        s_kkraw = sem("s_kkraw")
        s_sq = sem("s_sq")
        s_ssp = sem("s_ssp")
        s_ss = sem("s_ss")
        s_inv = sem("s_inv")
        s_invtp = sem("s_invtp")
        s_invt = sem("s_invt")
        s_invb = sem("s_invb")
        s_ln1 = sem("s_ln1")
        s_spl = sem("s_spl")
        s_wm = sem("s_wm")
        s_expwm = sem("s_expwm")
        s_kkb = sem("s_kkb")
        s_kfin = sem("s_kfin")
        s_rkf = sem("s_rkf")
        s_bonus = sem("s_bonus")
        s_vdram = sem("s_vdram")
        s_vb = sem("s_vb")
        s_vk = sem("s_vk")
        s_tkk = sem("s_tkk")
        s_u = sem("s_u")
        s_dvk = sem("s_dvk")
        s_state = sem("s_state")
        s_z = sem("s_z")
        s_h = sem("s_h")
        s_gelu = sem("s_gelu")
        s_vals = sem("s_vals")
        s_ex = sem("s_ex")
        s_sel = sem("s_sel")
        s_selp = sem("s_selp")
        s_selc = sem("s_selc")
        s_w2 = sem("s_w2")
        s_oh = sem("s_oh")
        s_s = sem("s_s")
        s_g = sem("s_g")
        s_up = sem("s_up")
        s_y = sem("s_y")
        s_yc = sem("s_yc")
        s_ysq = sem("s_ysq")
        s_yve = sem("s_yve")
        s_yrs = sem("s_yrs")
        s_yn = sem("s_yn")
        s_ytp = sem("s_ytp")
        s_yt = sem("s_yt")
        s_o = sem("s_o")
        s_thf = sem("s_thf")
        s_out = sem("s_out")
        s_stored = sem("s_stored")
        s_tick = sem("s_tick")
        s_dve = sem("s_dve")
        s_act = sem("s_act")
        s_pool = sem("s_pool")

        class Chain:

            def __init__(self, engine, semaphore, per_tile):
                self.engine, self.semaphore, self.per_tile = engine, semaphore, per_tile

            def start(self, t):
                self.base, self.count = t * self.per_tile, 0

            def inc(self, instruction):
                self.count += 1
                instruction.then_inc(self.semaphore, 1)

            def wait(self):
                self.engine.wait_ge(self.semaphore, self.base + self.count)

            def link(self, instruction):
                self.inc(instruction)
                self.wait()

            def settle(self):
                self.wait()
                self.engine.sem_inc(s_tick, 1)

            def end(self):
                assert self.count == self.per_tile, (self.semaphore, self.count)

        block = ctx.enter_context(nc.Block())

        @block.sync
        def _(sp):
            sp.dma_start(cst[:, :], params).then_inc(s_par, 16)
            sp.dma_start(wdown[:, :], down).then_inc(s_par, 16)
            sp.dma_start(wup[:, :], up).then_inc(s_par, 16)
            with sp.Fori(0, tiles) as t:
                sp.wait_ge(s_xfree, t + 1)
                sp.dma_start(x_in[:, :], bass.AP(x.tensor, t * (TOK * C), [[C, TOK], [1, C]])).then_inc(s_x, 16)
                sp.wait_ge(s_vt, t + 1)
                sp.dma_start(bass.AP(vscratch.tensor, 0, [[TOK, P], [P * TOK, HALVES], [1, TOK]]),
                             v(v_t, 0, (TOK, HALVES), (1, TOK))).then_inc(s_vdram, 16)
                sp.wait_ge(s_vdram, 16 * t + 16)
                sp.wait_ge(s_y, t + 1)
                for h in range(HH):
                    sp.dma_start(v(vk, 0, (N * TOK, HALVES), (1, N * TOK), p0=h * N, n=N),
                                 bass.AP(vscratch.tensor, h * N * TOK,
                                         [[0, N], [P * TOK, HALVES], [1, N * TOK]])).then_inc(s_vb, 16)
                sp.wait_ge(s_out, t + 1)
                sp.dma_start(bass.AP(out.tensor, t * (TOK * C), [[C, TOK], [1, C]]), y_out[:, :]).then_inc(s_stored, 16)
            sp.wait_ge(s_stored, 16 * tiles + 16)

        @block.gpsimd
        def _(pool):
            gp = nc.gpsimd
            chain = Chain(pool, s_pool, 2 + J + 0)
            pool.wait_ge(s_par, 48)
            with pool.Fori(0, tiles) as t:
                chain.start(t)
                pool.wait_ge(s_vare, t + 1)
                gp.tensor_tensor(rstd[:, :], vareps[:, :], c_("mhalf", 0, (1, 1)), ALU.pow).then_inc(s_rstd, 1)
                pool.wait_ge(s_ss, t + 1)
                gp.tensor_tensor(inv_n[:, :], ss[:, :], c_("mhalf", 0, (1, H)), ALU.pow).then_inc(s_inv, 1)
                pool.wait_ge(s_vb, 16 * HH * t + 16 * HH)
                pool.wait_ge(s_kfin, t + 1)
                for c in range(HALVES):
                    o = v(vk, c * N * TOK, (TOK, N), (1, TOK))
                    chain.inc(gp.tensor_tensor(o, o, v(k_fin, c * TOK, (0, N), (1, TOK)), ALU.mult))
                chain.wait()
                for j in range(J):
                    prev = (j - 1) % J
                    pool.wait_ge(s_state, J * t + j + 1)
                    chain.link(gp.tensor_tensor(v(t_d, 0, (B * N, HALVES), (N, B), (1, N)),
                                                v(hist, prev * SW, (B * N, HALVES), (N, B), (1, N)),
                                                v(expw, j, (TOK, HALVES), (J, B), (0, N)), ALU.mult))
                    gp.tensor_tensor(v(t_dvk, 0, (B * N, HALVES), (N, B), (1, N)),
                                     v(t_d, 0, (B * N, HALVES), (N, B), (1, N)),
                                     v(vk, j, (N * TOK, HALVES), (J, B), (TOK, N)), ALU.add).then_inc(s_dvk, 1)
                pool.wait_ge(s_state, J * t + J + 1)
                for c in range(HALVES):
                    i = gp.tensor_tensor(v(z, c * N * TOK, (TOK, N), (J, B), (1, J)),
                                         v(hist, c * B * N, (1, N), (N, B), (SW, J)),
                                         v(r_t, c * TOK, (0, N), (J, B), (1, J)), ALU.mult)
                i.then_inc(s_z, 1)
                pool.wait_ge(s_yve, t + 1)
                gp.tensor_tensor(yrs[:, :], yve[:, :], c_("mhalf", 0, (1, H)), ALU.pow).then_inc(s_yrs, 1)
                chain.end()

        @block.scalar
        def _(act):
            sc = nc.scalar
            chain = Chain(act, s_act, 2)
            act.wait_ge(s_par, 48)
            act.wait_ge(s_pre, 1)
            with act.Fori(0, tiles) as t:
                chain.start(t)
                act.wait_ge(s_xtp, t + 1)
                chain.link(sc.copy(v(xt, 0, (B * (J + 1), HALVES), (J + 1, B), (1, 1)),
                                   v(xt, J, (B * (J + 1), HALVES), (J + 1, B), (1, 1))))
                sc.copy(v(xt, 1, (B * (J + 1), HALVES), (J + 1, B), (1, J)),
                        v(ps_a0, 0, (TOK, HALVES), (J, B), (1, J)))
                sc.copy(xnt[:, :], v(ps_a0, 0, (1, HALVES * TOK))).then_inc(s_xt, 1)
                act.wait_ge(s_z, t + 1)
                act.wait_ge(s_q, t + 1)
                for m in range(4):
                    i = sc.activation(v(q_t, m * TOK, (1, TOK)), v(ps_h[0], m * TOK, (1, TOK)), ACT.Identity,
                                      bias=c_("bq", m, (1, 1)))
                i.then_inc(s_qt, 1)
                act.wait_ge(s_mixp, t + 1)
                sc.activation(mix[:, :], v(ps_a1, 0, (1, TOK)), ACT.Tanh).then_inc(s_mix, 1)
                act.wait_ge(s_scp, t + 1)
                sc.copy(v(scores, 0, (1, 512)), ps_s[0][:, :])
                sc.copy(v(scores, 512, (1, 512)), ps_s[1][:, :]).then_inc(s_scores, 1)
                act.wait_ge(s_p1, t + 1)
                sc.copy(r_t[:, :], v(ps_a0, 0, (1, 256)))
                sc.copy(k_t[:, :], v(ps_a0, 256, (1, 256)))
                sc.activation(tgate[:, :], v(ps_a1, 0, (1, TOK)), ACT.Tanh)
                sc.activation(v(low_a, 0, (1, TOK), n=64), v(ps_a1, TOK, (1, TOK), n=64), ACT.Tanh)
                sc.copy(v(low_a, 0, (1, TOK), p0=64, n=32), v(ps_a1, TOK, (1, TOK), p0=64, n=32))
                sc.activation(v(low_k, 0, (1, TOK), n=32), v(ps_a1, 2 * TOK, (1, TOK), n=32), ACT.Tanh)
                sc.copy(v(low_k, 0, (1, TOK), p0=32, n=16),
                        v(ps_a1, 2 * TOK, (1, TOK), p0=32, n=16)).then_inc(s_c1, 1)
                act.wait_ge(s_p2, t + 1)
                sc.copy(v_t[:, :], v(ps_a0, 0, (1, 256))).then_inc(s_vt, 1)
                sc.copy(v_tok[:, :], v(ps_a0, 256, (1, 256)))
                for c in range(HALVES):
                    sc.activation(v(absz, c * TOK, (1, TOK)), v(ps_a1, c * TOK, (1, TOK)), ACT.Abs,
                                  bias=c_("td", c, (1, 1)))
                    sc.activation(v(reluz, c * TOK, (1, TOK)), v(ps_a1, c * TOK, (1, TOK)), ACT.Relu,
                                  bias=v(ntd, c, (1, 1)), scale=-1.0)
                for c in range(HALVES):
                    i = sc.activation(v(tanh_a, c * TOK, (1, TOK)), v(ps_a1, 256 + c * TOK, (1, TOK)), ACT.Tanh,
                                      bias=v(hba, c, (1, 1)), scale=0.5)
                i.then_inc(s_c2, 1)
                act.wait_ge(s_p3, t + 1)
                for c in range(HALVES):
                    sc.activation(v(tanh_ma, c * TOK, (1, TOK)), v(ps_a0, c * TOK, (1, TOK)), ACT.Tanh,
                                  bias=v(hbma, c, (1, 1)), scale=0.5)
                    sc.activation(v(tanh_mk, c * TOK, (1, TOK)), v(ps_a0, 256 + c * TOK, (1, TOK)), ACT.Tanh,
                                  bias=v(hbmk, c, (1, 1)), scale=0.5)
                sc.copy(g_tok[:, :], v(ps_a1, 256, (1, 256))).then_inc(s_c3, 1)
                act.wait_ge(s_kkraw, t + 1)
                sc.activation(kk_sq[:, :], kk_raw[:, :], ACT.Square).then_inc(s_sq, 1)
                chain.link(sc.activation(absz[:, :], absz[:, :], ACT.Exp, scale=-1.0))
                sc.activation(absz[:, :], absz[:, :], ACT.Ln, bias=1.0).then_inc(s_ln1, 1)
                act.wait_ge(s_invtp, t + 1)
                sc.copy(v(inv_nt, 0, (1, TOK), n=H), v(ps_a0, 0, (1, TOK), n=H)).then_inc(s_invt, 1)
                act.wait_ge(s_spl, t + 1)
                sc.activation(expw[:, :], spl[:, :], ACT.Exp, bias=mhalf_b[:, :], scale=-1.0)
                act.wait_ge(s_wm, t + 1)
                sc.activation(expwm[:, :], wm[:, :], ACT.Exp).then_inc(s_expwm, 1)
                act.wait_ge(s_up, t + 1)
                for q in range(8):
                    act.wait_ge(s_h, 8 * t + q + 1)
                    sc.activation(v(gh, q * 512, (1, 512)), ps_h[q % 2][:, :], ACT.Gelu).then_inc(s_gelu, 1)
                act.wait_ge(s_vals, t + 1)
                sc.activation(ex[:, :], dif[:, :], ACT.Exp).then_inc(s_ex, 1)
                act.wait_ge(s_selp, t + 1)
                sc.copy(hi_t[:, :], v(ps_s[0], 0, (1, TOK), n=SEL))
                sc.copy(lo_t[:, :], v(ps_s[0], TOK, (1, TOK), n=SEL))
                sc.activation(w1_t[:, :], v(ps_s[0], 2 * TOK, (1, TOK), n=SEL), ACT.Copy,
                              scale=WSCALE).then_inc(s_selc, 1)
                act.wait_ge(s_yc, t + 1)
                sc.activation(ysq[:, :], yc[:, :], ACT.Square).then_inc(s_ysq, 1)
                act.wait_ge(s_ytp, t + 1)
                sc.copy(yt[:, :], v(ps_a0, 0, (1, 256))).then_inc(s_yt, 1)
                act.wait_ge(s_up, t + 2)
                sc.activation(th_f[:, :], v(ps_f, 0, (1, C)), ACT.Tanh, scale=0.5 / WSCALE).then_inc(s_thf, 1)
                chain.end()

        @block.vector
        def _(dve):
            ve = nc.vector
            ve.memset(xt[:, :], 0.0)
            ve.memset(v(hist, (J - 1) * SW, (1, SW)), 0.0)
            ve.memset(mhalf_b[:, :], -0.5)
            dve.wait_ge(s_par, 48)
            ve.tensor_scalar(ntd[:, :], c_("td", 0, (1, 2)), -1.0, None, ALU.mult)
            ve.tensor_scalar(hba[:, :], c_("ba", 0, (1, 2)), 0.5, None, ALU.mult)
            ve.tensor_scalar(hbma[:, :], c_("bma", 0, (1, 2)), 0.5, None, ALU.mult)
            ve.tensor_scalar(hbmk[:, :], c_("bmk", 0, (1, 2)), 0.5, None, ALU.mult)
            ve.tensor_copy(iota_e16[:, :], c_("iota_e", 0, (1, 256))).then_inc(s_pre, 1)
            dve.wait_ge(s_pre, 1)
            for s in (s_xfree, s_z, s_up, s_state, s_y):
                dve.sem_inc(s, 1)
            dve.sem_inc(s_stored, 16)
            chain = Chain(dve, s_dve, DVE_LINKS)
            with dve.Fori(0, tiles) as t:
                chain.start(t)
                link, inc, wait = chain.link, chain.inc, chain.wait
                dve.wait_ge(s_x, 16 * t + 16)
                inc(ve.bn_stats(stats[:, :], x_in[:, :]))
                chain.settle()
                link(ve.bn_aggr(meanvar[:, :], stats[:, :]))
                ve.tensor_scalar(vareps[:, :], v(meanvar, 1, (1, 1)), LN_EPS, None, ALU.add).then_inc(s_vare, 1)
                dve.wait_ge(s_rstd, t + 1)
                ve.tensor_scalar(xn[:, :], x_in[:, :], v(meanvar, 0, (1, 1)), rstd[:, :],
                                 ALU.subtract, ALU.mult).then_inc(s_xn, 1)
                dve.wait_ge(s_z, t + 1)
                dve.wait_ge(s_xt, t + 1)
                link(ve.tensor_tensor(v(xx, 0, (TOK, HALVES), (J, B), (1, J)),
                                      v(xt, 0, (B * (J + 1), HALVES), (J + 1, B), (1, J)),
                                      v(xt, 1, (B * (J + 1), HALVES), (J + 1, B), (1, J)), ALU.subtract))
                for c in range(HALVES):
                    i = ve.scalar_tensor_tensor(v(xxx, c * TOK, (1, TOK)), v(xx, c * TOK, (1, TOK)),
                                                c_("maax", c, (1, 1)), v(xnt, c * TOK, (1, TOK)), ALU.mult, ALU.add)
                i.then_inc(s_xxx, 1)
                dve.wait_ge(s_delta, t + 1)
                for f in range(4):
                    for c in range(HALVES):
                        i = ve.scalar_tensor_tensor(
                            v(xf, (f * 2 + c) * TOK, (1, TOK)),
                            v((ps_a0, ps_a1)[f // 2], (f % 2 * 2 + c) * TOK, (1, TOK)),
                            c_("maa", f * 2 + c, (1, 1)), v(xx, c * TOK, (1, TOK)), ALU.add, ALU.mult)
                link(i)
                ve.tensor_tensor(v(xf, 0, (256, 4), (1, 256)), v(xf, 0, (256, 4), (1, 256)),
                                 v(xnt, 0, (0, 4), (1, 256)), ALU.add).then_inc(s_xf, 1)
                dve.wait_ge(s_c2, t + 1)
                ve.tensor_scalar(a_t[:, :], tanh_a[:, :], 0.5, 0.5, ALU.mult, ALU.add)
                dve.wait_ge(s_c3, t + 1)
                link(ve.tensor_tensor(kk_raw[:, :], k_t[:, :], v(ps_h[0], 0, (1, 256)), ALU.add))
                ve.tensor_scalar(mk_t[:, :], tanh_mk[:, :], 0.5, 0.5, ALU.mult, ALU.add).then_inc(s_kkraw, 1)
                link(ve.tensor_scalar(kmul[:, :], tanh_ma[:, :], -1.0, None, ALU.add))
                link(ve.scalar_tensor_tensor(kmul[:, :], tanh_a[:, :], -1.0, kmul[:, :], ALU.add, ALU.mult))
                link(ve.tensor_scalar(kmul[:, :], kmul[:, :], -0.25, 1.0, ALU.mult, ALU.add))
                link(ve.tensor_tensor(kmul[:, :], kmul[:, :], k_t[:, :], ALU.mult))
                dve.wait_ge(s_ssp, t + 1)
                ve.tensor_scalar(ss[:, :], v(ps_h[1], 0, (1, H)), 1e-24, None, ALU.max).then_inc(s_ss, 1)
                dve.wait_ge(s_ln1, t + 1)
                ve.tensor_tensor(spl[:, :], reluz[:, :], absz[:, :], ALU.add).then_inc(s_spl, 1)
                dve.wait_ge(s_spl, t + 1)
                link(ve.tensor_scalar(wm[:, :], spl[:, :], -1.0, -0.5, ALU.mult, ALU.add))
                ve.tensor_tensor(wm[:, :], wm[:, :], mk_t[:, :], ALU.mult).then_inc(s_wm, 1)
                dve.wait_ge(s_expwm, t + 1)
                ve.tensor_tensor(k_fin[:, :], kmul[:, :], expwm[:, :], ALU.mult).then_inc(s_kfin, 1)
                dve.wait_ge(s_kfin, t + 1)
                for c in range(HALVES):
                    i = ve.scalar_tensor_tensor(v(rkf, c * TOK, (1, TOK)), v(r_t, c * TOK, (1, TOK)),
                                                c_("fa", c, (1, 1)), v(k_fin, c * TOK, (1, TOK)), ALU.mult, ALU.mult)
                i.then_inc(s_rkf, 1)
                dve.wait_ge(s_invb, t + 1)
                link(ve.tensor_tensor(kk[:, :], kk_raw[:, :], v(ps_a1, 0, (1, 256)), ALU.mult))
                ve.scalar_tensor_tensor(b_t[:, :], kk[:, :], -1.0, a_t[:, :], ALU.mult, ALU.mult).then_inc(s_kkb, 1)
                dve.wait_ge(s_bonus, t + 1)
                link(ve.tensor_tensor(v(bv, 0, (N, H), (1, N)), v(v_tok, 0, (N, H), (1, N)),
                                      v(ps_h[1], 0, (1, H), (0, N)), ALU.mult))
                dve.wait_ge(s_kkb, t + 1)

                def top_keys(g):
                    src = v(scores, g * NKEY, (1, NKEY))
                    s2 = v(scores2, (g % 2) * NKEY, (1, NKEY))
                    inc(ve.max(v(topv, g * 16, (1, 8)), src))
                    chain.settle()
                    inc(ve.match_replace(s2, v(topv, g * 16, (1, 8)), src, NEG))
                    ve.max_index(v(topi, g * 16, (1, 8)), v(topv, g * 16, (1, 8)), src)
                    chain.settle()
                    inc(ve.max(v(topv, g * 16 + 8, (1, 8)), s2))
                    chain.settle()
                    inc(ve.max_index(v(topi, g * 16 + 8, (1, 8)), v(topv, g * 16 + 8, (1, 8)), s2))

                def candidates():
                    wait()
                    link(ve.tensor_copy(topif[:, :], topi[:, :]))
                    link(ve.tensor_scalar(v(hi_f, 0, (16, FH), (1, 16)), v(topif, 16, (32, FH), (1, 16)), 31.5,
                                          2016.0, ALU.is_gt, ALU.mult))
                    link(ve.tensor_tensor(v(topif, 16, (32, FH), (1, 16)), v(topif, 16, (32, FH), (1, 16)),
                                          v(hi_f, 0, (16, FH), (1, 16)), ALU.add))
                    link(ve.tensor_scalar(v(topif, 0, (32, FH), (1, 16)), v(topif, 0, (32, FH), (1, 16)), 32.0,
                                          None, ALU.mult))
                    for dst, src in ((cand, topv), (candi, topif)):
                        for i0, ni, nj, at in ((0, 1, 10, 0), (1, 1, 5, 10), (2, 1, 3, 15), (3, 2, 2, 18), (5, 5, 1, 22)):
                            i = ve.tensor_tensor(v(dst, at, (NCAND, FH), (nj, ni), (1, nj)),
                                                 v(src, i0, (32, FH), (1, ni), (0, nj)),
                                                 v(src, 16, (32, FH), (0, ni), (1, nj)), ALU.add)
                    link(i)

                def top_pairs(h):
                    src = v(cand, h * NCAND, (1, NCAND))
                    inc(ve.max(v(vals, h * 16, (1, 8)), src))
                    chain.settle()
                    inc(ve.match_replace(cand2[:, :], v(vals, h * 16, (1, 8)), src, NEG))
                    ve.max_index(v(pos, h * 16, (1, 8)), v(vals, h * 16, (1, 8)), src)
                    chain.settle()
                    inc(ve.max(v(vals, h * 16 + 8, (1, 8)), cand2[:, :]))
                    chain.settle()
                    inc(ve.max_index(v(pos, h * 16 + 8, (1, 8)), v(vals, h * 16 + 8, (1, 8)), cand2[:, :]))

                def weights():
                    wait()
                    ve.tensor_tensor(v(dif, 0, (TOPK, FH), (1, TOPK)), v(vals, 0, (16, FH), (1, TOPK)),
                                     v(vals, 0, (16, FH), (0, TOPK)), ALU.subtract).then_inc(s_vals, 1)
                    link(ve.tensor_copy(posf[:, :], pos[:, :]))
                    grid = v(eqp, 0, (TOPK * NCAND, 4), (NCAND, TOPK), (1, NCAND))
                    for h in (0, 4):
                        link(ve.tensor_tensor(grid, v(posf, 16 * h, (16, 4), (1, TOPK), (0, NCAND)),
                                              c_("iota_c", 0, (0, 4), (0, TOPK), (1, NCAND)), ALU.is_equal))
                        link(ve.tensor_tensor(grid, grid, v(candi, h * NCAND, (NCAND, 4), (0, TOPK), (1, NCAND)),
                                              ALU.mult))
                        link(ve.tensor_reduce(v(sel, h * TOPK, (TOPK, 4), (1, TOPK)), grid, AX, ALU.add))
                    link(ve.tensor_copy(sel_i[:, :], sel[:, :]))
                    ve.tensor_scalar(sel_lo[:, :], sel_i[:, :], 31, None, ALU.bitwise_and)
                    link(ve.tensor_scalar(sel_hi[:, :], sel_i[:, :], 5, None, ALU.logical_shift_right))
                    ve.tensor_copy(lof[:, :], sel_lo[:, :])
                    ve.tensor_copy(hif[:, :], sel_hi[:, :])
                    dve.wait_ge(s_ex, t + 1)
                    link(ve.tensor_reduce(sume[:, :], v(ex, 0, (TOPK, FH), (1, TOPK)), AX, ALU.add))
                    link(ve.reciprocal(rsum[:, :], sume[:, :]))
                    ve.tensor_tensor(v(wsel, 0, (TOPK, FH), (1, TOPK)), v(ex, 0, (TOPK, FH), (1, TOPK)),
                                     v(rsum, 0, (1, FH), (0, TOPK)), ALU.mult).then_inc(s_sel, 1)

                for j in range(J):
                    prev = (j - 1) % J
                    state = lambda tensor, off=0: v(tensor, off, (B * N, HALVES), (N, B), (1, N))
                    of_step = lambda tensor: v(tensor, j, (TOK, HALVES), (J, B), (0, N))
                    dve.wait_ge(s_state, J * t + j + 1)
                    ve.tensor_tensor(state(t_kk), state(hist, prev * SW), of_step(kk), ALU.mult).then_inc(s_tkk, 1)
                    if j < 16:
                        if j == 0:
                            dve.wait_ge(s_scores, t + 1)
                            dve.sem_inc(s_tick, 1)
                        top_keys(j)
                    if j == 16:
                        candidates()
                    if 17 <= j < 25:
                        top_pairs(j - 17)
                    if j == 25:
                        weights()
                    dve.wait_ge(s_u, J * t + j + 1)
                    link(ve.tensor_tensor(state(t_o), state(ps_u), of_step(b_t), ALU.mult))
                    dve.wait_ge(s_dvk, J * t + j + 1)
                    ve.tensor_tensor(v(hist, j * SW, (1, SW)), t_o[:, :], t_dvk[:, :], ALU.add).then_inc(s_state, 1)

                dve.wait_ge(s_selc, t + 1)
                ve.scalar_tensor_tensor(w2_t[:, :], v(ps_s[0], 2 * TOK, (1, TOK), n=SEL), WSCALE, w1_t[:, :],
                                        ALU.mult, ALU.subtract).then_inc(s_w2, 1)
                dve.wait_ge(s_w2, t + 1)

                def one_hots(k):
                    i = k % 2
                    if k >= 2:
                        dve.wait_ge(s_s, NCH * t + k - 1)
                    pairs = lambda tensor, n: v(tensor, k * CH, (2, CH // 2), (0, n), (1, 2), n=SEL)
                    full = lambda tensor, n: v(tensor, 0, (2 * n, CH // 2), (2, n), (1, 2), n=SEL)
                    iota = lambda n: v(iota_e16, 0, (0, CH // 2), (2, n), (1, 2), n=SEL)
                    link(ve.tensor_tensor(full(oh_e[i], ER), iota(ER), pairs(lo_t, ER), ALU.is_equal))
                    ve.tensor_tensor(full(oh_a[i], P), iota(P), pairs(hi_t, P), ALU.is_equal)
                    ve.tensor_tensor(full(oh_1[i], ER), full(oh_e[i], ER), pairs(w1_t, ER), ALU.mult)
                    ve.tensor_tensor(full(oh_2[i], ER), full(oh_e[i], ER), pairs(w2_t, ER), ALU.mult).then_inc(s_oh, 1)

                def weigh(k):
                    dve.wait_ge(s_s, NCH * t + k + 1)
                    g = v(gh, k * CH, (TOK, ER), (1, CH))
                    ve.tensor_tensor(g, g, v(ps_s[k % 2], 0, (1, ER), (ER, CH)), ALU.mult).then_inc(s_g, 1)

                one_hots(0)
                one_hots(1)
                dve.wait_ge(s_y, t + 2)
                heads = lambda tensor, off=0: v(tensor, off, (N, H), (1, N))
                per_head = lambda tensor: v(tensor, 0, (1, H), (0, N))
                link(ve.tensor_reduce(ysum[:, :], heads(ps_f, 256), AX, ALU.add))
                link(ve.tensor_scalar(ymean[:, :], ysum[:, :], 1.0 / N, None, ALU.mult))
                ve.tensor_tensor(heads(yc), heads(ps_f, 256), per_head(ymean), ALU.subtract).then_inc(s_yc, 1)
                dve.wait_ge(s_gelu, 8 * t + 8)
                for k in range(NCH):
                    weigh(k)
                    if k + 2 < NCH:
                        one_hots(k + 2)
                    if k == 0:
                        dve.wait_ge(s_ysq, t + 1)
                        link(ve.tensor_reduce(yvs[:, :], heads(ysq), AX, ALU.add))
                        ve.tensor_scalar(yve[:, :], yvs[:, :], 1.0 / N, GN_EPS, ALU.mult, ALU.add).then_inc(s_yve, 1)
                    if k == 2:
                        dve.wait_ge(s_yrs, t + 1)
                        link(ve.tensor_tensor(heads(yn), heads(yc), per_head(yrs), ALU.mult))
                        link(ve.tensor_tensor(yn2[:, :], yn[:, :], c_("lnw", 0, (1, C)), ALU.mult))
                        link(ve.tensor_tensor(yn[:, :], yn2[:, :], c_("lnb", 0, (1, C)), ALU.add))
                        link(ve.tensor_tensor(yn2[:, :], yn[:, :], bv[:, :], ALU.add))
                        ve.tensor_tensor(yn[:, :], yn2[:, :], g_tok[:, :], ALU.mult).then_inc(s_yn, 1)
                dve.wait_ge(s_thf, t + 1)
                link(ve.tensor_scalar(sg_f[:, :], th_f[:, :], 0.5, 0.5, ALU.mult, ALU.add))
                link(ve.scalar_tensor_tensor(silu_f[:, :], v(ps_f, 0, (1, C)), 1.0 / WSCALE, sg_f[:, :],
                                             ALU.mult, ALU.mult))
                dve.wait_ge(s_o, t + 1)
                link(ve.tensor_tensor(o_s[:, :], v(ps_a1, 0, (1, C)), silu_f[:, :], ALU.mult))
                dve.wait_ge(s_stored, 16 * t + 16)
                ve.tensor_tensor(y_out[:, :], o_s[:, :], x_in[:, :], ALU.add).then_inc(s_out, 1)
                dve.wait_ge(s_out, t + 1)
                dve.sem_inc(s_xfree, 1)
                chain.end()

        @block.tensor
        def _(pe):
            te = nc.tensor

            def mm(o, lhs, rhs, first=True, last=True):
                return te.matmul(o, lhs, rhs, start=first, stop=last)

            pe.wait_ge(s_par, 48)
            with pe.Fori(0, tiles) as t:
                pe.wait_ge(s_xn, t + 1)
                for c in range(HALVES):
                    i = te.transpose(v(ps_a0, c * TOK, (1, TOK)), v(xn, c * P, (1, P)), c_("ident", 0, (1, P)))
                i.then_inc(s_xtp, 1)
                pe.wait_ge(s_xt, t + 1)
                for m in range(4):
                    for c in range(HALVES):
                        i = mm(v(ps_h[0], m * TOK, (1, TOK)), c_("wq", c * 512 + m * P, (1, P)),
                               v(xnt, c * TOK, (1, TOK)), c == 0, c == 1)
                i.then_inc(s_q, 1)
                pe.wait_ge(s_xxx, t + 1)
                for c in range(HALVES):
                    i = mm(v(ps_a1, 0, (1, TOK)), c_("w1", c * P, (1, P)), v(xxx, c * TOK, (1, TOK)), c == 0, c == 1)
                i.then_inc(s_mixp, 1)
                pe.wait_ge(s_qt, t + 1)
                for m in range(4):
                    i = mm(v(ps_s[m // 2], (m % 2) * 256, (1, 256)), v(q_t, m * TOK, (1, TOK)), c_("kbd", 0, (1, 256)))
                i.then_inc(s_scp, 1)
                pe.wait_ge(s_mix, t + 1)
                for f in range(4):
                    for c in range(HALVES):
                        i = mm(v((ps_a0, ps_a1)[f // 2], (f % 2 * 2 + c) * TOK, (1, TOK)),
                               c_("w2", f * 256 + c * P, (1, P)), mix[:, :])
                i.then_inc(s_delta, 1)

                def project(o, off, name, f, m0, m, width):
                    for c in range(HALVES):
                        i = mm(v(o, off, (1, TOK), n=m), c_(name, c * width + m0, (1, m)),
                               v(xf, (f * 2 + c) * TOK, (1, TOK)), c == 0, c == 1)
                    return i

                pe.wait_ge(s_xf, t + 1)
                for c in range(HALVES):
                    project(ps_a0, c * TOK, "wr", 0, c * P, P, 256)
                for c in range(HALVES):
                    project(ps_a0, 256 + c * TOK, "wk", 2, c * P, P, 256)
                project(ps_a1, 0, "gw1", 0, 0, 128, 128)
                project(ps_a1, TOK, "lowa", 1, 0, 96, 96)
                project(ps_a1, 2 * TOK, "lowk", 2, 0, 48, 48).then_inc(s_p1, 1)
                pe.wait_ge(s_c1, t + 1)
                for c in range(HALVES):
                    project(ps_a0, c * TOK, "wv", 3, c * P, P, 256)
                for c in range(HALVES):
                    mm(v(ps_a0, 256, (1, 256)), v(xf, (6 + c) * TOK, (1, TOK)), c_("wv", c * 256, (1, 256)),
                       c == 0, c == 1)
                for o, name in ((0, "dec2"), (256, "aaa2")):
                    for c in range(HALVES):
                        i = mm(v(ps_a1, o + c * TOK, (1, TOK)), c_(name, c * P, (1, P), n=96),
                               v(low_a, 0, (1, TOK), n=96))
                i.then_inc(s_p2, 1)
                for c in range(HALVES):
                    mm(v(ps_h[0], c * TOK, (1, TOK)), c_("kkk2", c * P, (1, P), n=48), v(low_k, 0, (1, TOK), n=48))
                pe.wait_ge(s_c2, t + 1)
                for c in range(HALVES):
                    mm(v(ps_a0, c * TOK, (1, TOK)), c_("ma2", c * P, (1, P), n=96), v(low_a, 0, (1, TOK), n=96))
                for c in range(HALVES):
                    mm(v(ps_a0, 256 + c * TOK, (1, TOK)), c_("mk2", c * P, (1, P), n=48), v(low_k, 0, (1, TOK), n=48))
                mm(v(ps_a1, 256, (1, 256)), tgate[:, :], c_("gw2", 0, (1, 256))).then_inc(s_p3, 1)
                pe.wait_ge(s_sq, t + 1)
                for c in range(HALVES):
                    i = mm(v(ps_h[1], c * HH, (1, HH)), v(kk_sq, c * TOK, (1, TOK)), c_("headcol", 0, (1, HH)))
                i.then_inc(s_ssp, 1)
                pe.wait_ge(s_inv, t + 1)
                te.transpose(v(ps_a0, 0, (1, TOK), n=H), inv_n[:, :], c_("ident", 0, (1, P))).then_inc(s_invtp, 1)
                pe.wait_ge(s_invt, t + 1)
                for c in range(HALVES):
                    i = mm(v(ps_a1, c * TOK, (1, TOK)), c_("headrow", c * P, (1, P), n=H), v(inv_nt, 0, (1, TOK), n=H))
                i.then_inc(s_invb, 1)
                pe.wait_ge(s_rkf, t + 1)
                for c in range(HALVES):
                    i = mm(v(ps_h[1], c * HH, (1, HH)), v(rkf, c * TOK, (1, TOK)), c_("headcol", 0, (1, HH)))
                i.then_inc(s_bonus, 1)
                for j in range(J):
                    pe.wait_ge(s_tkk, J * t + j + 1)
                    mm(v(ps_u, 0, (1, SW)), c_("headones", 0, (1, P)), t_kk[:, :]).then_inc(s_u, 1)
                    if j < 8:
                        if j >= 2:
                            pe.wait_ge(s_gelu, 8 * t + j - 1)
                        for e in range(4):
                            for c in range(HALVES):
                                i = mm(v(ps_h[j % 2], e * TOK, (1, TOK)),
                                       v(wdown, (c * ER + j * 4 + e) * P, (1, P)),
                                       v(xnt, c * TOK, (1, TOK)), c == 0, c == 1)
                        i.then_inc(s_h, 1)
                    if j == 26:
                        pe.wait_ge(s_sel, t + 1)
                        for m, src in enumerate((hif, lof, wsel)):
                            i = te.transpose(v(ps_s[0], m * TOK, (1, TOK), n=SEL), src[:, :], c_("ident", 0, (1, P)))
                        i.then_inc(s_selp, 1)
                def expert_weights(k):
                    pe.wait_ge(s_oh, NCH * t + k + 1)
                    if k >= 2:
                        pe.wait_ge(s_g, NCH * t + k - 1)
                    for m in range(CH):
                        o = v(ps_s[k % 2], m * ER, (1, ER))
                        lhs = v(oh_a[k % 2], (m // 2) * 2 * P + m % 2, (2, P), n=SEL)
                        at = (m // 2) * 2 * ER + m % 2
                        mm(o, lhs, v(oh_1[k % 2], at, (2, ER), n=SEL), True, False)
                        i = mm(o, lhs, v(oh_2[k % 2], at, (2, ER), n=SEL), False, True)
                    i.then_inc(s_s, 1)

                expert_weights(0)
                pe.wait_ge(s_z, t + 2)
                for c in range(HALVES):
                    for m in range(N):
                        i = mm(v(ps_f, 256 + c * P + m, (N, HH)), v(z, (c * N + m) * TOK, (1, TOK)),
                               c_("headcol", 0, (1, HH)))
                i.then_inc(s_y, 1)
                for k in range(1, NCH):
                    expert_weights(k)
                pe.wait_ge(s_yn, t + 1)
                for c in range(HALVES):
                    i = te.transpose(v(ps_a0, c * TOK, (1, TOK)), v(yn, c * P, (1, P)), c_("ident", 0, (1, P)))
                i.then_inc(s_ytp, 1)
                pe.wait_ge(s_yt, t + 1)
                for c in range(HALVES):
                    i = mm(v(ps_a1, 0, (1, C)), v(yt, c * TOK, (1, TOK)), c_("wo", c * 256, (1, 256)), c == 0, c == 1)
                i.then_inc(s_o, 1)
                pe.wait_ge(s_g, NCH * t + NCH)
                for e in range(ER):
                    i = mm(v(ps_f, 0, (1, C)), v(gh, e * TOK, (1, TOK)), v(wup, e * C, (1, C)), e == 0, e == ER - 1)
                i.then_inc(s_up, 1)



def pack(inputs):
    import numpy as np
    g = {k: np.asarray(a) for k, a in inputs.items()}
    p = "L0_attn_"
    z = np.zeros((P, NCONST), g[p + "x"].dtype)

    def put(name, a, r0=0, off=0):
        a = np.asarray(a)
        z[r0:r0 + a.shape[0], COL[name] + off:COL[name] + off + a.shape[1]] = a

    def halves(name, wt):
        for c in range(2):
            put(name, wt[c * P:(c + 1) * P], off=c * wt.shape[1])

    halves("w1", g[p + "time_maa_w1"].T)
    for f in range(4):
        put("w2", g[p + "time_maa_w2"][f].T, r0=32 * f, off=256 * f)
    halves("wr", g[p + "receptance"].T)
    halves("wk", g[p + "key_w"].T)
    halves("wv", g[p + "value"].T)
    halves("gw1", g[p + "gate_w1"].T)
    halves("lowa", np.concatenate([g[p + "time_decay_w1"], g[p + "time_aaa_w1"], g[p + "ma_w1"]], 0).T)
    pad = np.zeros((16, C), z.dtype)
    halves("lowk", np.concatenate([g[p + "time_kkk_w1"], pad, g[p + "mk_w1"]], 0).T)
    put("dec2", g[p + "time_decay_w2"].T, 0)
    put("aaa2", g[p + "time_aaa_w2"].T, 64)
    put("ma2", g[p + "ma_w2"].T, 80)
    put("kkk2", g[p + "time_kkk_w2"].T, 0)
    put("mk2", g[p + "mk_w2"].T, 32)
    put("gw2", g[p + "gate_w2"].T)
    halves("wq", g["L0_ffn_Wq"])
    for a in range(2):
        put("kbd", g["L0_ffn_K1"].T, 64 * a, 128 * a)
        put("kbd", g["L0_ffn_K2"].T, 64 * a + 32, 128 * a + 64)
    halves("wo", g[p + "output"].T)
    put("ident", np.eye(P))
    put("headones", np.kron(np.eye(HH), np.ones((N, N))))
    put("headcol", np.kron(np.eye(HH), np.ones((N, 1))))
    for c in range(2):
        put("headrow", np.kron(np.eye(HH), np.ones((1, N))), 8 * c, P * c)
    cols = lambda a: np.asarray(a).reshape(-1, P).T
    put("maax", cols(g[p + "time_maa_x"]))
    put("maa", cols(g[p + "time_maa"]))
    put("td", cols(g[p + "time_decay"]))
    put("ba", cols(g[p + "time_aaaaa"]))
    put("bma", cols(g[p + "time_misc_a"]))
    put("bmk", cols(g[p + "time_misc_k"]))
    put("fa", cols(g[p + "time_faaaa"]))
    put("bq", cols(g["L0_ffn_bq"]))
    put("lnw", np.broadcast_to(g[p + "ln_w"], (P, C)))
    put("lnb", np.broadcast_to(g[p + "ln_b"], (P, C)))
    put("iota_e", np.broadcast_to(np.repeat(np.arange(P), 2), (P, 2 * P)))
    put("iota_c", np.broadcast_to(np.arange(NCAND), (P, NCAND)))
    put("mhalf", np.full((P, 16), -0.5))
    def experts(w):
        return w[:NKEY * NKEY].reshape(NKEY, 2, ER, C).transpose(1, 0, 2, 3)
    up = np.ascontiguousarray(experts(g["L0_ffn_W_up"]).reshape(P, ER * C))
    down = experts(g["L0_ffn_W_down"]).reshape(P, ER, 2, P).transpose(3, 2, 1, 0)
    return z, np.ascontiguousarray(down.reshape(P, 2 * ER * P)), up


def kernel(**inputs):
    import numpy as _np
    import concourse.bacc as _bacc
    from concourse.bass_utils import run_bass_kernel_spmd as _run

    x = _np.asarray(inputs["L0_attn_x"])
    tiles = x.shape[1] // J
    xt = _np.ascontiguousarray(x.reshape(B, tiles, J, C).transpose(1, 0, 2, 3).reshape(tiles * TOK, C))
    params, down, up = pack(inputs)
    arrays = {"in_x": xt, "in_params": params, "in_down": down, "in_up": up}
    nc = _bacc.Bacc("TRN2", target_bir_lowering=False, num_devices=1)
    aps = [nc.dram_tensor(n, a.shape, F32, kind="ExternalInput").ap() for n, a in arrays.items()]
    vs = nc.dram_tensor("v_scratch", (C, TOK), F32, kind="Internal").ap()
    out = nc.dram_tensor("out_0", (tiles * TOK, C), F32, kind="ExternalOutput").ap()
    build(nc, *aps, vs, out, tiles)
    r = _run(nc, [arrays], core_ids=[0])
    y = _np.asarray(r.results[0]["out_0"])
    return y.reshape(tiles, B, J, C).transpose(1, 0, 2, 3).reshape(x.shape)
```

```python
from contextlib import ExitStack

import concourse.bass as bass
from concourse import mybir

P = 128
B = 4
C = 256
HALVES = 2
J = 32
TOK = B * J
H = 16
N = 16
HH = 8
FH = 8
NKEY = 64
TOPK = 10
PAIRS = [(0, 10), (1, 5), (2, 3), (3, 2), (4, 2), (5, 1), (6, 1), (7, 1), (8, 1), (9, 1)]
NCAND = sum(n for _, n in PAIRS)
SEL = FH * TOPK
ER = 32
CH = 16
NCH = TOK // CH
DVE_LINKS = (11, 149, 15, 3)
WSCALE = 8192.0
NEG = -3.0e38
LN_EPS = 1e-5
GN_EPS = 0.00064

F32 = mybir.dt.float32
F16 = mybir.dt.float16
U32 = mybir.dt.uint32
I32 = mybir.dt.int32
ALU = mybir.AluOpType
ACT = mybir.ActivationFunctionType
AX = mybir.AxisListType.X

LAYOUT = [
    ("w1", 2 * 128), ("w2", 4 * 256), ("wr", 2 * 256), ("wk", 2 * 256), ("wv", 2 * 256), ("gw1", 2 * 128),
    ("lowa", 2 * 96), ("lowk", 2 * 48), ("dec2", 256), ("aaa2", 256), ("ma2", 256), ("kkk2", 256), ("mk2", 256),
    ("gw2", 256), ("wq", 2 * 512), ("kbd", 256), ("wo", 2 * 256), ("ident", 128), ("headones", 128),
    ("headcol", 8), ("headrow", 2 * 128), ("maax", 2), ("maa", 8), ("td", 2), ("ba", 2), ("bma", 2), ("bmk", 2),
    ("fa", 2), ("bq", 4), ("lnw", 256), ("lnb", 256), ("iota_c", NCAND + 1), ("mhalf", 16),
]
COL = {}
_at = 0
for _n, _w in LAYOUT:
    COL[_n] = _at
    _at += _w
NCONST = _at


class Part:

    def __init__(self, tensor, at, width):
        self.tensor, self.at, self.width = tensor, at, width

    def __getitem__(self, key):
        return self.tensor[:, self.at:self.at + self.width]


def v(t, off, *dims, p0=0, n=P):
    if isinstance(t, Part):
        off, t = off + t.at, t.tensor
    a = t[p0:p0 + n, :]
    return bass.AP(a.tensor, a.offset + off, [list(a.ap[0])] + [list(d) for d in dims])


def build(nc, x, params, down, up, iota_e, vscratch, out, tiles):
    with ExitStack() as ctx:
        def sb(name, width, dt=F32, parts=P):
            return ctx.enter_context(nc.sbuf_tensor(name, [parts, width], dt))

        def sem(name):
            return ctx.enter_context(nc.semaphore(name))

        def bank(name):
            return ctx.enter_context(nc.psum_tensor(name, [P, 512], F32))

        ps_u = bank("ps_u")
        ps_a0, ps_a1 = bank("ps_a0"), bank("ps_a1")
        ps_h = [bank("ps_h0"), bank("ps_h1")]
        ps_s = [bank("ps_s0"), bank("ps_s1")]
        ps_f = bank("ps_f")

        cst = sb("cst", NCONST)
        wdown = sb("wdown", HALVES * ER * P)
        wup = sb("wup", ER * C)
        iota_e16 = sb("iota_e16", 256, F16)
        ntd = sb("ntd", 2)
        hba = sb("hba", 2)
        hbma = sb("hbma", 2)
        hbmk = sb("hbmk", 2)
        mhalf_b = sb("mhalf_b", 1)

        def c_(name, off, *dims, p0=0, n=P):
            return v(cst, COL[name] + off, *dims, p0=p0, n=n)

        def both(name, width):
            return [sb(f"{name}{i}", width) for i in range(2)]

        W2 = HALVES * TOK
        x_in = sb("x_in", C)
        stats = sb("stats", 6)
        meanvar = sb("meanvar", 2)
        vareps = sb("vareps", 1)
        rstd = sb("rstd", 1)
        xt = sb("xt", HALVES * B * (J + 1))
        xnt = both("xnt", W2)
        xh = sb("xh", W2)
        xx = sb("xx", W2)
        tgate = Part(xx, 0, TOK)
        low_a = Part(xx, TOK, TOK)
        low_k = mix = sb("low_k", TOK)
        xxx = sb("xxx", W2)
        v_t = kk_sq = rkf = xxx
        xf = sb("xf", 4 * W2)
        r_t = both("r_t", W2)
        k_t = sb("k_t", W2)
        bv = both("bv", C)
        g_tok = both("g_tok", C)
        absz = sb("absz", W2)
        wm = expwm = absz
        reluz = sb("reluz", W2)
        spl = reluz
        tanh_m = sb("tanh_m", 2 * W2)
        tanh_ma, tanh_mk = Part(tanh_m, 0, W2), Part(tanh_m, W2, W2)
        mk_t = tanh_mk
        q_t = tanh_m
        ss = sb("ss", H)
        inv_n = sb("inv_n", H)
        inv_nt = sb("inv_nt", TOK)
        kk = both("kk", W2)
        b_t = tanh_a = both("b_t", W2)
        expw = both("expw", W2)
        k_fin = sb("k_fin", W2)
        scores = sb("scores", FH * 2 * NKEY)
        scores2 = sb("scores2", 2 * NKEY)

        SW = HALVES * B * N
        JH = J // 2
        hist = sb("hist", J * SW)
        carry = sb("carry", SW)
        vk = [sb(f"vk{i}", HALVES * N * B * JH) for i in range(2)]
        t_kk = sb("t_kk", SW)
        t_dvk = sb("t_dvk", SW)

        CARRIED = [(B * N, HALVES), (N, B), (1, N)]
        IN_HIST = [(N * TOK, HALVES), (J, B), (TOK, N)]

        def state_after(step):
            return v(carry, 0, *CARRIED) if step in (-1, J - 1) else v(hist, step, *IN_HIST)

        topv = sb("topv", 16 * 16)
        topi = sb("topi", 16 * 16, U32)
        topif = Part(scores, 0, 256)
        hi_f = Part(scores, 256, FH * 16)
        cand = sb("cand", FH * NCAND)
        candi = sb("candi", FH * NCAND)
        cand2 = sb("cand2", NCAND)
        vals = sb("vals", FH * 16)
        pos = sb("pos", FH * 16, U32)
        posf = sb("posf", FH * 16)
        eqp = xf
        sel = sb("sel", SEL)
        sel_i = sb("sel_i", SEL, I32)
        sel_lo = sb("sel_lo", SEL, I32)
        sel_hi = sb("sel_hi", SEL, I32)
        lof = sel
        hif = sb("hif", SEL)
        dif = sb("dif", SEL)
        ex = sb("ex", SEL)
        sume = sb("sume", FH)
        rsum = sb("rsum", FH)
        wsel = sb("wsel", SEL)
        hi_t = sb("hi_t", TOK, F16, SEL)
        lo_t = sb("lo_t", TOK, F16, SEL)
        w1_t = sb("w1_t", TOK, F16, SEL)
        w2_t = sb("w2_t", TOK, F16, SEL)
        oh_a = [sb(f"oh_a{i}", CH * P, F16, SEL) for i in range(2)]
        oh_e = sb("oh_e", CH * ER, F16, SEL)
        oh_1 = [sb(f"oh_1{i}", CH * ER, F16, SEL) for i in range(2)]
        oh_2 = [sb(f"oh_2{i}", CH * ER, F16, SEL) for i in range(2)]
        gh = sb("gh", ER * TOK)

        ysum = sb("ysum", H)
        ymean = sb("ymean", H)
        yc = sb("yc", C)
        ysq = sb("ysq", C)
        yt = ysq
        yvs = sb("yvs", H)
        yve = sb("yve", H)
        yrs = sb("yrs", H)
        yn = sb("yn", C)
        o_att = sb("o_att", C)
        sg_f = sb("sg_f", C)
        y_out = sb("y_out", C)

        s_par = sem("s_par")
        s_pre = sem("s_pre")
        s_x = sem("s_x")
        s_xr = sem("s_xr")
        s_vare = sem("s_vare")
        s_rstd = sem("s_rstd")
        s_xn = sem("s_xn")
        s_xtp = sem("s_xtp")
        s_xt = sem("s_xt")
        s_xh = sem("s_xh")
        s_xxx = sem("s_xxx")
        s_mixp = sem("s_mixp")
        s_mix = sem("s_mix")
        s_delta = sem("s_delta")
        s_xf = sem("s_xf")
        s_q = sem("s_q")
        s_qt = sem("s_qt")
        s_scp = sem("s_scp")
        s_scores = sem("s_scores")
        s_p1 = sem("s_p1")
        s_c1 = sem("s_c1")
        s_p2 = sem("s_p2")
        s_vt = sem("s_vt")
        s_c2 = sem("s_c2")
        s_p3 = sem("s_p3")
        s_c3 = sem("s_c3")
        s_kkraw = sem("s_kkraw")
        s_sq = sem("s_sq")
        s_ssp = sem("s_ssp")
        s_ss = sem("s_ss")
        s_inv = sem("s_inv")
        s_invtp = sem("s_invtp")
        s_invt = sem("s_invt")
        s_invb = sem("s_invb")
        s_ln1 = sem("s_ln1")
        s_spl = sem("s_spl")
        s_expw = sem("s_expw")
        s_wm = sem("s_wm")
        s_expwm = sem("s_expwm")
        s_kkb = sem("s_kkb")
        s_kfin = sem("s_kfin")
        s_rkf = sem("s_rkf")
        s_bonus = sem("s_bonus")
        s_vdram = sem("s_vdram")
        s_vb = [sem("s_vb0"), sem("s_vb1")]
        s_vk = sem("s_vk")
        s_tkk = sem("s_tkk")
        s_u = sem("s_u")
        s_dvk = sem("s_dvk")
        s_state = sem("s_state")
        s_z = sem("s_z")
        s_h = sem("s_h")
        s_gelu = sem("s_gelu")
        s_vals = sem("s_vals")
        s_ex = sem("s_ex")
        s_sel = sem("s_sel")
        s_selp = sem("s_selp")
        s_selc = sem("s_selc")
        s_w2 = sem("s_w2")
        s_oh = sem("s_oh")
        s_s = sem("s_s")
        s_g = sem("s_g")
        s_up = sem("s_up")
        s_y = sem("s_y")
        s_yc = sem("s_yc")
        s_ysq = sem("s_ysq")
        s_yve = sem("s_yve")
        s_yrs = sem("s_yrs")
        s_yn = sem("s_yn")
        s_ytp = sem("s_ytp")
        s_yt = sem("s_yt")
        s_o = sem("s_o")
        s_oatt = sem("s_oatt")
        s_thf = sem("s_thf")
        s_out = sem("s_out")
        s_stored = sem("s_stored")
        s_tick = sem("s_tick")
        s_da = sem("s_da")
        s_db = sem("s_db")
        s_dc = sem("s_dc")
        s_df = sem("s_df")
        s_act = sem("s_act")
        s_pd = sem("s_pd")

        def need(engine, semaphore, count):
            if not (isinstance(count, int) and count <= 0):
                engine.wait_ge(semaphore, count)

        class Chain:

            def __init__(self, engine, semaphore, per_tile):
                self.engine, self.semaphore, self.per_tile = engine, semaphore, per_tile

            def start(self, t):
                self.base, self.count = t * self.per_tile, 0

            def inc(self, instruction):
                self.count += 1
                instruction.then_inc(self.semaphore, 1)

            def wait(self):
                self.engine.wait_ge(self.semaphore, self.base + self.count)

            def link(self, instruction):
                self.inc(instruction)
                self.wait()

            def settle(self):
                self.wait()
                self.engine.sem_inc(s_tick, 1)

            def end(self):
                assert self.count == self.per_tile, (self.semaphore, self.count)

        def rounds(engine, body):
            def at(t):
                body(t, t % 2, t + 1 in range(tiles), t in range(tiles), t - 1 in range(tiles), t - 2 in range(tiles))

            for t in (-1, 0, 1):
                at(t)
            with engine.Fori(2, tiles - 2, 2) as t:
                body(t, 0, True, True, True, True)
                body(t + 1, 1, True, True, True, True)
            for t in range(tiles - 2, tiles + 2):
                at(t)

        block = ctx.enter_context(nc.Block())

        @block.sync
        def _(sp):
            def tile_of(dram, t):
                return bass.AP(dram.tensor, t * (TOK * C), [[C, TOK], [1, C]])

            HALF = HALVES * N * B * JH

            def broadcast_v(t, i):
                for h in range(HH):
                    sp.dma_start(v(vk[i], 0, (1, HALF), p0=h * N, n=N),
                                 bass.AP(vscratch.tensor, (h * 2 + i) * HALF, [[0, N], [1, HALF]])
                                 ).then_inc(s_vb[i], 16)

            def body(t, par, a, b, c, f):
                if b:
                    need(sp, s_dvk, J * t)
                    broadcast_v(t, 1)
                if f:
                    sp.wait_ge(s_out, t - 1)
                    sp.dma_start(tile_of(out, t - 2), y_out[:, :]).then_inc(s_stored, 16)
                if c:
                    need(sp, s_stored, 16 * (t - 1))
                    sp.dma_start(y_out[:, :], tile_of(x, t - 1)).then_inc(s_xr, 16)
                if a:
                    if not isinstance(t, int) or t + 2 < tiles:
                        sp.wait_ge(s_xtp, t + 2)
                        sp.dma_start(x_in[:, :], tile_of(x, t + 2)).then_inc(s_x, 16)
                    if b:
                        sp.wait_ge(s_vb[1], 16 * HH * t + 16 * HH)
                    sp.wait_ge(s_vt, t + 2)
                    for i in range(2):
                        for m in range(HALVES):
                            sp.dma_start(
                                bass.AP(vscratch.tensor, i * HALF + m * (N * B * JH),
                                        [[2 * HALF, HH], [B * JH, N], [JH, B], [1, JH]]),
                                v(v_t, m * TOK + i * JH, (J, B), (1, JH))).then_inc(s_vdram, 16)
                    sp.wait_ge(s_vdram, 64 * t + 128)
                    sp.sem_inc(s_tick, 1)
                    need(sp, s_dvk, J * t + JH)
                    broadcast_v(t + 1, 0)

            sp.dma_start(cst[:, :], params).then_inc(s_par, 16)
            sp.dma_start(v(gh, 0, (1, 256)), iota_e).then_inc(s_par, 16)
            sp.dma_start(x_in[:, :], tile_of(x, 0)).then_inc(s_x, 16)
            sp.dma_start(wdown[:, :], down).then_inc(s_par, 16)
            sp.dma_start(wup[:, :], up).then_inc(s_par, 16)
            rounds(sp, body)
            sp.wait_ge(s_stored, 16 * tiles)

        @block.gpsimd
        def _(pool):
            gp = nc.gpsimd

            def body(t, par, a, b, c, f):
                def times_k(i, piece):
                    m, v0 = piece // 4, piece % 4 * 4
                    o = v(vk[i], (m * N + v0) * B * JH, (B * JH, 4), (JH, B), (1, JH))
                    gp.tensor_tensor(o, o, v(k_fin, m * TOK + i * JH, (0, 4), (J, B), (1, JH)),
                                     ALU.mult).then_inc(s_vk, 1)

                def times_r(m, j0, n):
                    o = v(hist, m * N * TOK + j0, (J, B), (TOK, N), (1, n))
                    gp.tensor_tensor(o, o, v(r_t[par], m * TOK + j0, (J, B), (0, N), (1, n)), ALU.mult)

                for j in range(J):
                    if b:
                        need(pool, s_state, J * t + j)
                        if j == 0:
                            pool.wait_ge(s_expw, t + 1)
                        gp.tensor_tensor(v(t_dvk, 0, *CARRIED), state_after(j - 1),
                                         v(expw[par], j, (TOK, HALVES), (J, B), (0, N)), ALU.mult).then_inc(s_pd, 1)
                        if j % JH == 0:
                            pool.wait_ge(s_vk, 16 * t + 8 + 8 * (j // JH))
                        pool.wait_ge(s_pd, J * t + j + 1)
                        gp.tensor_tensor(v(t_dvk, 0, *CARRIED), v(t_dvk, 0, *CARRIED),
                                         v(vk[j // JH], j % JH, (N * B * JH, HALVES), (JH, B), (B * JH, N)),
                                         ALU.add).then_inc(s_dvk, 1)
                        if j in (10, 11, 17, 18, 25, 26):
                            q, m = {10: (0, 0), 11: (0, 1), 17: (1, 0), 18: (1, 1), 25: (2, 0), 26: (2, 1)}[j]
                            pool.wait_ge(s_tkk, J * t + 8 * q + 9)
                            times_r(m, 8 * q, 8)
                        if j == 31:
                            pool.wait_ge(s_tkk, J * t + J)
                            times_r(0, 24, 7)
                            times_r(1, 24, 7)
                    if c and j == 0:
                        pool.wait_ge(s_state, J * t)
                        gp.tensor_tensor(v(hist, J - 1, *IN_HIST), v(carry, 0, *CARRIED),
                                         v(r_t[1 - par], J - 1, (TOK, HALVES), (J, B), (0, N)),
                                         ALU.mult).then_inc(s_z, 1)
                    if a and j == 0:
                        pool.wait_ge(s_vare, t + 2)
                        gp.tensor_tensor(rstd[:, :], vareps[:, :], c_("mhalf", 0, (1, 1)), ALU.pow).then_inc(s_rstd, 1)
                    if b and 2 <= j < 10:
                        if j == 2:
                            pool.wait_ge(s_vb[1], 16 * HH * t + 16 * HH)
                            pool.wait_ge(s_kfin, t + 1)
                        times_k(1, j - 2)
                    if c and j == 4:
                        pool.wait_ge(s_yve, t)
                        gp.tensor_tensor(yrs[:, :], yve[:, :], c_("mhalf", 0, (1, H)), ALU.pow).then_inc(s_yrs, 1)
                    if a and j == 15:
                        pool.wait_ge(s_ss, t + 2)
                        gp.tensor_tensor(inv_n[:, :], ss[:, :], c_("mhalf", 0, (1, H)), ALU.pow).then_inc(s_inv, 1)
                    if a and 20 <= j < 28:
                        if j == 20:
                            pool.wait_ge(s_vb[0], 16 * HH * t + 32 * HH)
                            pool.wait_ge(s_kfin, t + 2)
                        times_k(0, j - 20)

            pool.wait_ge(s_par, 64)
            rounds(pool, body)

        @block.scalar
        def _(act):
            sc = nc.scalar
            chain = Chain(act, s_act, 2)

            def body(t, par, a, b, c, f):
                def gelu(q):
                    if c:
                        if q == 0:
                            need(act, s_up, t - 1)
                        act.wait_ge(s_h, 8 * t + (q - 7))
                        sc.activation(v(gh, q * 512, (1, 512)), ps_h[q % 2][:, :], ACT.Gelu).then_inc(s_gelu, 1)

                nxt = 1 - par
                if f:
                    act.wait_ge(s_up, t - 1)
                    sc.activation(sg_f[:, :], v(ps_f, 0, (1, C)), ACT.Tanh, scale=0.5 / WSCALE).then_inc(s_thf, 1)
                gelu(0)
                if c:
                    act.wait_ge(s_yc, t)
                    sc.activation(ysq[:, :], yc[:, :], ACT.Square).then_inc(s_ysq, 1)
                gelu(1)
                if a:
                    chain.start(t + 1)
                    act.wait_ge(s_xtp, t + 2)
                    chain.link(sc.copy(v(xt, 0, (B * (J + 1), HALVES), (J + 1, B), (1, 1)),
                                       v(xt, J, (B * (J + 1), HALVES), (J + 1, B), (1, 1))))
                    sc.copy(v(xt, 1, (B * (J + 1), HALVES), (J + 1, B), (1, J)),
                            v(ps_a0, 0, (TOK, HALVES), (J, B), (1, J)))
                    need(act, s_xh, t)
                    sc.copy(xnt[nxt][:, :], v(ps_a0, 0, (1, W2))).then_inc(s_xt, 1)
                gelu(2)
                gelu(3)
                if a:
                    act.wait_ge(s_mixp, t + 2)
                    sc.activation(mix[:, :], v(ps_a1, 0, (1, TOK)), ACT.Tanh).then_inc(s_mix, 1)
                gelu(4)
                if c:
                    act.wait_ge(s_ytp, t)
                    sc.copy(yt[:, :], v(ps_s[1], 256, (1, 256))).then_inc(s_yt, 1)
                gelu(5)
                if c:
                    act.wait_ge(s_o, t)
                    need(act, s_out, t - 1)
                    sc.copy(o_att[:, :], v(ps_s[1], 0, (1, C))).then_inc(s_oatt, 1)
                if a:
                    act.wait_ge(s_p1, t + 2)
                    need(act, s_z, t)
                    sc.copy(r_t[nxt][:, :], v(ps_a0, 0, (1, 256)))
                    sc.copy(k_t[:, :], v(ps_a0, 256, (1, 256)))
                    sc.activation(tgate[:, :], v(ps_a1, 0, (1, TOK)), ACT.Tanh)
                    sc.activation(v(low_a, 0, (1, TOK), n=64), v(ps_a1, TOK, (1, TOK), n=64), ACT.Tanh)
                    sc.copy(v(low_a, 0, (1, TOK), p0=64, n=32), v(ps_a1, TOK, (1, TOK), p0=64, n=32))
                    sc.activation(v(low_k, 0, (1, TOK), n=32), v(ps_a1, 2 * TOK, (1, TOK), n=32), ACT.Tanh)
                    sc.copy(v(low_k, 0, (1, TOK), p0=32, n=16),
                            v(ps_a1, 2 * TOK, (1, TOK), p0=32, n=16)).then_inc(s_c1, 1)
                gelu(6)
                if a:
                    act.wait_ge(s_p2, t + 2)
                    sc.copy(v_t[:, :], v(ps_a0, 0, (1, 256))).then_inc(s_vt, 1)
                    need(act, s_yn, t)
                    sc.copy(bv[nxt][:, :], v(ps_a0, 256, (1, 256)))
                    for m in range(HALVES):
                        sc.activation(v(absz, m * TOK, (1, TOK)), v(ps_a1, m * TOK, (1, TOK)), ACT.Abs,
                                      bias=c_("td", m, (1, 1)))
                        sc.activation(v(reluz, m * TOK, (1, TOK)), v(ps_a1, m * TOK, (1, TOK)), ACT.Relu,
                                      bias=v(ntd, m, (1, 1)), scale=-1.0)
                    for m in range(HALVES):
                        i = sc.activation(v(tanh_a[nxt], m * TOK, (1, TOK)), v(ps_a1, 256 + m * TOK, (1, TOK)), ACT.Tanh,
                                          bias=v(hba, m, (1, 1)), scale=0.5)
                    i.then_inc(s_c2, 1)
                gelu(7)
                if a:
                    act.wait_ge(s_p3, t + 2)
                    for m in range(HALVES):
                        sc.activation(v(tanh_ma, m * TOK, (1, TOK)), v(ps_a0, m * TOK, (1, TOK)), ACT.Tanh,
                                      bias=v(hbma, m, (1, 1)), scale=0.5)
                        sc.activation(v(tanh_mk, m * TOK, (1, TOK)), v(ps_a0, 256 + m * TOK, (1, TOK)), ACT.Tanh,
                                      bias=v(hbmk, m, (1, 1)), scale=0.5)
                    sc.copy(kk[nxt][:, :], v(ps_a1, 0, (1, 256)))
                    sc.copy(g_tok[nxt][:, :], v(ps_a1, 256, (1, 256))).then_inc(s_c3, 1)
                if b:
                    need(act, s_h, 8 * t)
                    sc.copy(xh[:, :], xnt[par][:, :]).then_inc(s_xh, 1)
                if a:
                    act.wait_ge(s_kkraw, t + 2)
                    act.wait_ge(s_vdram, 64 * t + 128)
                    sc.activation(kk_sq[:, :], kk[nxt][:, :], ACT.Square).then_inc(s_sq, 1)
                    chain.link(sc.activation(absz[:, :], absz[:, :], ACT.Exp, scale=-1.0))
                    sc.activation(absz[:, :], absz[:, :], ACT.Ln, bias=1.0).then_inc(s_ln1, 1)
                    act.wait_ge(s_invtp, t + 2)
                    sc.copy(v(inv_nt, 0, (1, TOK), n=H), v(ps_a1, 0, (1, TOK), n=H)).then_inc(s_invt, 1)
                    act.wait_ge(s_spl, t + 2)
                    need(act, s_dvk, J * t)
                    sc.activation(expw[nxt][:, :], spl[:, :], ACT.Exp, bias=mhalf_b[:, :], scale=-1.0).then_inc(s_expw, 1)
                    act.wait_ge(s_wm, t + 2)
                    sc.activation(expwm[:, :], wm[:, :], ACT.Exp).then_inc(s_expwm, 1)
                    act.wait_ge(s_q, t + 2)
                    for m in range(4):
                        i = sc.activation(v(q_t, m * TOK, (1, TOK)), v(ps_a0, m * TOK, (1, TOK)), ACT.Identity,
                                          bias=c_("bq", m, (1, 1)))
                    i.then_inc(s_qt, 1)
                if b:
                    act.wait_ge(s_vals, t + 1)
                    sc.activation(ex[:, :], dif[:, :], ACT.Exp).then_inc(s_ex, 1)
                if a:
                    act.wait_ge(s_scp, t + 2)
                    sc.copy(v(scores, 0, (1, 512)), ps_a0[:, :])
                    sc.copy(v(scores, 512, (1, 512)), ps_a1[:, :]).then_inc(s_scores, 1)
                if b:
                    act.wait_ge(s_selp, t + 1)
                    need(act, s_oh, NCH * t)
                    sc.copy(hi_t[:, :], v(ps_s[0], 0, (1, TOK), n=SEL))
                    sc.copy(lo_t[:, :], v(ps_s[0], TOK, (1, TOK), n=SEL))
                    sc.activation(w1_t[:, :], v(ps_s[0], 2 * TOK, (1, TOK), n=SEL), ACT.Copy,
                                  scale=WSCALE).then_inc(s_selc, 1)

            act.wait_ge(s_par, 64)
            act.wait_ge(s_pre, 1)
            rounds(act, body)

        @block.vector
        def _(dve):
            ve = nc.vector
            ve.memset(xt[:, :], 0.0)
            ve.memset(carry[:, :], 0.0)
            ve.memset(mhalf_b[:, :], -0.5)
            dve.wait_ge(s_par, 64)
            ve.tensor_scalar(ntd[:, :], c_("td", 0, (1, 2)), -1.0, None, ALU.mult)
            ve.tensor_scalar(hba[:, :], c_("ba", 0, (1, 2)), 0.5, None, ALU.mult)
            ve.tensor_scalar(hbma[:, :], c_("bma", 0, (1, 2)), 0.5, None, ALU.mult)
            ve.tensor_scalar(hbmk[:, :], c_("bmk", 0, (1, 2)), 0.5, None, ALU.mult)
            ve.tensor_copy(iota_e16[:, :], v(gh, 0, (1, 256))).then_inc(s_pre, 1)
            dve.wait_ge(s_pre, 1)
            ca, cb, cc, cf = (Chain(dve, s, n) for s, n in zip((s_da, s_db, s_dc, s_df), DVE_LINKS))
            heads = lambda tensor, off=0: v(tensor, off, (N, H), (1, N))
            per_head = lambda tensor: v(tensor, 0, (1, H), (0, N))

            def a_stats(n):
                dve.wait_ge(s_x, 16 * n + 16)
                ca.inc(ve.bn_stats(stats[:, :], x_in[:, :]))
                ca.settle()
                ca.link(ve.bn_aggr(meanvar[:, :], stats[:, :]))
                ve.tensor_scalar(vareps[:, :], v(meanvar, 1, (1, 1)), LN_EPS, None, ALU.add).then_inc(s_vare, 1)

            def a_normalize(n):
                dve.wait_ge(s_rstd, n + 1)
                ve.tensor_scalar(x_in[:, :], x_in[:, :], v(meanvar, 0, (1, 1)), rstd[:, :],
                                 ALU.subtract, ALU.mult).then_inc(s_xn, 1)

            def a_shift(n, p):
                dve.wait_ge(s_xt, n + 1)
                ca.link(ve.tensor_tensor(v(xx, 0, (TOK, HALVES), (J, B), (1, J)),
                                         v(xt, 0, (B * (J + 1), HALVES), (J + 1, B), (1, J)),
                                         v(xt, 1, (B * (J + 1), HALVES), (J + 1, B), (1, J)), ALU.subtract))
                for m in range(HALVES):
                    i = ve.scalar_tensor_tensor(v(xxx, m * TOK, (1, TOK)), v(xx, m * TOK, (1, TOK)),
                                                c_("maax", m, (1, 1)), v(xnt[p], m * TOK, (1, TOK)),
                                                ALU.mult, ALU.add)
                i.then_inc(s_xxx, 1)

            def a_mixed(n):
                dve.wait_ge(s_delta, n + 1)
                for f in range(4):
                    for m in range(HALVES):
                        i = ve.scalar_tensor_tensor(
                            v(xf, (f * 2 + m) * TOK, (1, TOK)),
                            v((ps_a0, ps_a1)[f // 2], (f % 2 * 2 + m) * TOK, (1, TOK)),
                            c_("maa", f * 2 + m, (1, 1)), v(xx, m * TOK, (1, TOK)), ALU.add, ALU.mult)
                ca.inc(i)

            def a_mixed_add(n, p):
                ca.wait()
                ve.tensor_tensor(v(xf, 0, (256, 4), (1, 256)), v(xf, 0, (256, 4), (1, 256)),
                                 v(xnt[p], 0, (0, 4), (1, 256)), ALU.add).then_inc(s_xf, 1)

            def a_kk(n, p):
                dve.wait_ge(s_c3, n + 1)
                ve.tensor_tensor(kk[p][:, :], k_t[:, :], kk[p][:, :], ALU.add).then_inc(s_kkraw, 1)
                ve.tensor_scalar(mk_t[:, :], tanh_mk[:, :], 0.5, 0.5, ALU.mult, ALU.add)

            def a_kmul(n, p):
                need(dve, s_vk, 16 * n)
                ca.link(ve.tensor_scalar(k_fin[:, :], tanh_ma[:, :], -1.0, None, ALU.add))
                ca.link(ve.scalar_tensor_tensor(k_fin[:, :], tanh_a[p][:, :], -1.0, k_fin[:, :], ALU.add, ALU.mult))
                ve.tensor_scalar(b_t[p][:, :], tanh_a[p][:, :], 0.5, 0.5, ALU.mult, ALU.add)
                ca.link(ve.tensor_scalar(k_fin[:, :], k_fin[:, :], -0.25, 1.0, ALU.mult, ALU.add))
                ca.inc(ve.tensor_tensor(k_fin[:, :], k_fin[:, :], k_t[:, :], ALU.mult))

            def a_norm(n):
                dve.wait_ge(s_ssp, n + 1)
                ve.tensor_scalar(ss[:, :], v(ps_a0, 0, (1, H)), 1e-24, None, ALU.max).then_inc(s_ss, 1)

            def a_decay(n):
                dve.wait_ge(s_ln1, n + 1)
                ve.tensor_tensor(spl[:, :], reluz[:, :], absz[:, :], ALU.add).then_inc(s_spl, 1)
                dve.wait_ge(s_spl, n + 1)
                ca.link(ve.tensor_scalar(wm[:, :], spl[:, :], -1.0, -0.5, ALU.mult, ALU.add))
                ve.tensor_tensor(wm[:, :], wm[:, :], mk_t[:, :], ALU.mult).then_inc(s_wm, 1)

            def a_kk_b(n, p):
                dve.wait_ge(s_invb, n + 1)
                ca.link(ve.tensor_tensor(kk[p][:, :], kk[p][:, :], v(ps_a0, 0, (1, 256)), ALU.mult))
                ve.scalar_tensor_tensor(b_t[p][:, :], kk[p][:, :], -1.0, b_t[p][:, :],
                                        ALU.mult, ALU.mult).then_inc(s_kkb, 1)

            def a_kfin(n, p):
                dve.wait_ge(s_expwm, n + 1)
                ve.tensor_tensor(k_fin[:, :], k_fin[:, :], expwm[:, :], ALU.mult).then_inc(s_kfin, 1)
                dve.wait_ge(s_kfin, n + 1)
                for m in range(HALVES):
                    i = ve.scalar_tensor_tensor(v(rkf, m * TOK, (1, TOK)), v(r_t[p], m * TOK, (1, TOK)),
                                                c_("fa", m, (1, 1)), v(k_fin, m * TOK, (1, TOK)), ALU.mult, ALU.mult)
                i.then_inc(s_rkf, 1)

            def a_bonus(n, p):
                dve.wait_ge(s_bonus, n + 1)
                ca.inc(ve.tensor_tensor(heads(bv[p]), heads(bv[p]), v(ps_a1, 0, (1, H), (0, N)), ALU.mult))

            def top_keys(n, g):
                if g == 0:
                    dve.wait_ge(s_scores, n + 1)
                    dve.sem_inc(s_tick, 1)
                src = v(scores, g * NKEY, (1, NKEY))
                s2 = v(scores2, (g % 2) * NKEY, (1, NKEY))
                cb.inc(ve.max(v(topv, g * 16, (1, 8)), src))
                cb.settle()
                cb.inc(ve.match_replace(s2, v(topv, g * 16, (1, 8)), src, NEG))
                ve.max_index(v(topi, g * 16, (1, 8)), v(topv, g * 16, (1, 8)), src)
                cb.settle()
                cb.inc(ve.max(v(topv, g * 16 + 8, (1, 8)), s2))
                cb.settle()
                cb.inc(ve.max_index(v(topi, g * 16 + 8, (1, 8)), v(topv, g * 16 + 8, (1, 8)), s2))

            def candidates():
                cb.wait()
                cb.link(ve.tensor_copy(topif[:, :], topi[:, :]))
                cb.link(ve.tensor_scalar(v(hi_f, 0, (16, FH), (1, 16)), v(topif, 16, (32, FH), (1, 16)), 31.5,
                                         2016.0, ALU.is_gt, ALU.mult))
                ve.tensor_scalar(v(topif, 0, (32, FH), (1, 16)), v(topif, 0, (32, FH), (1, 16)), 32.0,
                                 None, ALU.mult)
                cb.link(ve.tensor_tensor(v(topif, 16, (32, FH), (1, 16)), v(topif, 16, (32, FH), (1, 16)),
                                         v(hi_f, 0, (16, FH), (1, 16)), ALU.add))
                for dst, src in ((cand, topv), (candi, topif)):
                    for i0, ni, nj, at in ((0, 1, 10, 0), (1, 1, 5, 10), (2, 1, 3, 15), (3, 2, 2, 18), (5, 5, 1, 22)):
                        i = ve.tensor_tensor(v(dst, at, (NCAND, FH), (nj, ni), (1, nj)),
                                             v(src, i0, (32, FH), (1, ni), (0, nj)),
                                             v(src, 16, (32, FH), (0, ni), (1, nj)), ALU.add)
                cb.inc(i)

            def top_pairs(h):
                src = v(cand, h * NCAND, (1, NCAND))
                cb.settle()
                cb.inc(ve.max(v(vals, h * 16, (1, 8)), src))
                cb.settle()
                cb.inc(ve.match_replace(cand2[:, :], v(vals, h * 16, (1, 8)), src, NEG))
                ve.max_index(v(pos, h * 16, (1, 8)), v(vals, h * 16, (1, 8)), src)
                cb.settle()
                cb.inc(ve.max(v(vals, h * 16 + 8, (1, 8)), cand2[:, :]))
                cb.settle()
                cb.inc(ve.max_index(v(pos, h * 16 + 8, (1, 8)), v(vals, h * 16 + 8, (1, 8)), cand2[:, :]))

            def differences():
                cb.wait()
                ve.tensor_tensor(v(dif, 0, (TOPK, FH), (1, TOPK)), v(vals, 0, (16, FH), (1, TOPK)),
                                 v(vals, 0, (16, FH), (0, TOPK)), ALU.subtract).then_inc(s_vals, 1)
                cb.inc(ve.tensor_copy(posf[:, :], pos[:, :]))

            def codes(h):
                grid = v(eqp, 0, (TOPK * NCAND, 2), (NCAND, TOPK), (1, NCAND))
                cb.wait()
                cb.link(ve.tensor_tensor(grid, v(posf, 16 * h, (16, 2), (1, TOPK), (0, NCAND)),
                                         c_("iota_c", 0, (0, 2), (0, TOPK), (1, NCAND)), ALU.is_equal))
                cb.link(ve.tensor_tensor(grid, grid, v(candi, h * NCAND, (NCAND, 2), (0, TOPK), (1, NCAND)), ALU.mult))
                cb.inc(ve.tensor_reduce(v(sel, h * TOPK, (TOPK, 2), (1, TOPK)), grid, AX, ALU.add))

            def coordinates(n):
                cb.wait()
                cb.link(ve.tensor_copy(sel_i[:, :], sel[:, :]))
                ve.tensor_scalar(sel_lo[:, :], sel_i[:, :], 31, None, ALU.bitwise_and)
                cb.link(ve.tensor_scalar(sel_hi[:, :], sel_i[:, :], 5, None, ALU.logical_shift_right))
                ve.tensor_copy(lof[:, :], sel_lo[:, :])
                ve.tensor_copy(hif[:, :], sel_hi[:, :])

            def softmax(n):
                dve.wait_ge(s_ex, n + 1)
                cb.link(ve.tensor_reduce(sume[:, :], v(ex, 0, (TOPK, FH), (1, TOPK)), AX, ALU.add))
                cb.link(ve.reciprocal(rsum[:, :], sume[:, :]))
                ve.tensor_tensor(v(wsel, 0, (TOPK, FH), (1, TOPK)), v(ex, 0, (TOPK, FH), (1, TOPK)),
                                 v(rsum, 0, (1, FH), (0, TOPK)), ALU.mult).then_inc(s_sel, 1)

            def second_part(n):
                dve.wait_ge(s_selc, n + 1)
                ve.scalar_tensor_tensor(w2_t[:, :], v(ps_s[0], 2 * TOK, (1, TOK), n=SEL), WSCALE, w1_t[:, :],
                                        ALU.mult, ALU.subtract).then_inc(s_w2, 1)

            def one_hots(n, k):
                i = k % 2
                if k == 0:
                    dve.wait_ge(s_w2, n + 1)
                if k >= 2:
                    dve.wait_ge(s_s, NCH * n + k - 1)
                need(dve, s_oh, NCH * n + k)
                pairs = lambda tensor, w: v(tensor, k * CH, (2, CH // 2), (0, w), (1, 2), n=SEL)
                full = lambda tensor, w: v(tensor, 0, (2 * w, CH // 2), (2, w), (1, 2), n=SEL)
                iota = lambda w: v(iota_e16, 0, (0, CH // 2), (2, w), (1, 2), n=SEL)
                cc.inc(ve.tensor_tensor(full(oh_e, ER), iota(ER), pairs(lo_t, ER), ALU.is_equal))
                ve.tensor_tensor(full(oh_a[i], P), iota(P), pairs(hi_t, P), ALU.is_equal)
                cc.wait()
                ve.tensor_tensor(full(oh_1[i], ER), full(oh_e, ER), pairs(w1_t, ER), ALU.mult)
                ve.tensor_tensor(full(oh_2[i], ER), full(oh_e, ER), pairs(w2_t, ER), ALU.mult).then_inc(s_oh, 1)

            def weigh(n, k):
                if k == 0:
                    dve.wait_ge(s_gelu, 8 * n + 8)
                dve.wait_ge(s_s, NCH * n + k + 1)
                g = v(gh, k * CH, (TOK, ER), (1, CH))
                ve.tensor_tensor(g, g, v(ps_s[k % 2], 0, (1, ER), (ER, CH)), ALU.mult).then_inc(s_g, 1)

            def group_mean(n):
                dve.wait_ge(s_y, n + 1)
                cc.link(ve.tensor_reduce(ysum[:, :], heads(ps_s[1]), AX, ALU.add))
                cc.link(ve.tensor_scalar(ymean[:, :], ysum[:, :], 1.0 / N, None, ALU.mult))
                ve.tensor_tensor(heads(yc), heads(ps_s[1]), per_head(ymean), ALU.subtract).then_inc(s_yc, 1)

            def group_var(n):
                dve.wait_ge(s_ysq, n + 1)
                cc.link(ve.tensor_reduce(yvs[:, :], heads(ysq), AX, ALU.add))
                ve.tensor_scalar(yve[:, :], yvs[:, :], 1.0 / N, GN_EPS, ALU.mult, ALU.add).then_inc(s_yve, 1)

            def gated(n, p):
                dve.wait_ge(s_yrs, n + 1)
                cc.link(ve.tensor_tensor(heads(yn), heads(yc), per_head(yrs), ALU.mult))
                cc.link(ve.tensor_tensor(yn[:, :], yn[:, :], c_("lnw", 0, (1, C)), ALU.mult))
                cc.link(ve.tensor_tensor(yn[:, :], yn[:, :], c_("lnb", 0, (1, C)), ALU.add))
                cc.link(ve.tensor_tensor(yn[:, :], yn[:, :], bv[p][:, :], ALU.add))
                ve.tensor_tensor(yn[:, :], yn[:, :], g_tok[p][:, :], ALU.mult).then_inc(s_yn, 1)

            def combine(n):
                dve.wait_ge(s_thf, n + 1)
                cf.link(ve.tensor_scalar(sg_f[:, :], sg_f[:, :], 0.5, 0.5, ALU.mult, ALU.add))
                cf.link(ve.scalar_tensor_tensor(sg_f[:, :], v(ps_f, 0, (1, C)), 1.0 / WSCALE, sg_f[:, :],
                                                ALU.mult, ALU.mult))
                dve.wait_ge(s_oatt, n + 1)
                cf.link(ve.tensor_tensor(sg_f[:, :], o_att[:, :], sg_f[:, :], ALU.mult))
                dve.wait_ge(s_xr, 16 * n + 16)
                ve.tensor_tensor(y_out[:, :], y_out[:, :], sg_f[:, :], ALU.add).then_inc(s_out, 1)

            def body(t, par, a, b, c, f):
                nxt = 1 - par
                for chain, on, n in ((ca, a, t + 1), (cb, b, t), (cc, c, t - 1), (cf, f, t - 2)):
                    if on:
                        chain.start(n)

                def beside(j):
                    if f and j == 0:
                        combine(t - 2)
                    if b:
                        if j < 16:
                            top_keys(t, j)
                        if j == 16:
                            candidates()
                        if 17 <= j < 23:
                            for h in {17: (0,), 18: (1,), 19: (2, 3), 20: (4,), 21: (5,), 22: (6, 7)}[j]:
                                top_pairs(h)
                        if j == 23:
                            differences()
                        if 24 <= j < 28:
                            if j == 24 and a:
                                dve.wait_ge(s_p2, t + 2)
                            codes(2 * (j - 24))
                        if j == 28:
                            coordinates(t)
                            softmax(t)
                        if j == 31:
                            second_part(t)
                    if c:
                        if j == 1:
                            group_mean(t - 1)
                        if j == 3:
                            group_var(t - 1)
                        if j == 5:
                            gated(t - 1, nxt)
                        for k, at in enumerate((11, 12, 14, 16, 18, 20, 22, 24)):
                            if j == at:
                                weigh(t - 1, k)
                        for k, at in enumerate((2, 4, 11, 12, 14, 16, 18, 20)):
                            if j == at:
                                one_hots(t - 1, k)
                    if a:
                        if j == 0:
                            a_stats(t + 1)
                        if j == 1:
                            a_normalize(t + 1)
                        if j == 3:
                            a_shift(t + 1, nxt)
                        if j == 6:
                            a_mixed(t + 1)
                        if j == 7:
                            a_mixed_add(t + 1, nxt)
                        if j == 13:
                            a_kk(t + 1, nxt)
                            a_kmul(t + 1, nxt)
                        if j == 15:
                            a_norm(t + 1)
                        if j == 17:
                            a_decay(t + 1)
                        if j == 18:
                            a_kk_b(t + 1, nxt)
                        if j == 19:
                            a_kfin(t + 1, nxt)
                        if j == 21:
                            a_bonus(t + 1, nxt)

                for j in range(J):
                    if b:
                        carried = lambda tensor: v(tensor, 0, *CARRIED)
                        of_step = lambda tensor: v(tensor[par], j, (TOK, HALVES), (J, B), (0, N))
                        if j == 0:
                            dve.wait_ge(s_kkb, t + 1)
                        need(dve, s_state, J * t + j)
                        ve.tensor_tensor(carried(t_kk), state_after(j - 1), of_step(kk), ALU.mult).then_inc(s_tkk, 1)
                    beside(j)
                    if b:
                        dve.wait_ge(s_u, J * t + j + 1)
                        if j == 0:
                            need(dve, s_y, t)
                        if j == J - 1:
                            dve.wait_ge(s_dvk, J * t + J)
                        cb.link(ve.tensor_tensor(state_after(j), carried(ps_u), of_step(b_t), ALU.mult))
                        dve.wait_ge(s_dvk, J * t + j + 1)
                        ve.tensor_tensor(state_after(j), state_after(j), carried(t_dvk), ALU.add).then_inc(s_state, 1)
                for chain, on in ((ca, a), (cb, b), (cc, c), (cf, f)):
                    if on:
                        chain.end()

            rounds(dve, body)

        @block.tensor
        def _(pe):
            te = nc.tensor

            def mm(o, lhs, rhs, first=True, last=True):
                return te.matmul(o, lhs, rhs, start=first, stop=last)

            ident = c_("ident", 0, (1, P))

            def a_transpose(n):
                pe.wait_ge(s_xn, n + 1)
                need(pe, s_scores, n)
                for m in range(HALVES):
                    i = te.transpose(v(ps_a0, m * TOK, (1, TOK)), v(x_in, m * P, (1, P)), ident)
                i.then_inc(s_xtp, 1)

            def a_mix(n):
                pe.wait_ge(s_xxx, n + 1)
                for m in range(HALVES):
                    i = mm(v(ps_a1, 0, (1, TOK)), c_("w1", m * P, (1, P)), v(xxx, m * TOK, (1, TOK)), m == 0, m == 1)
                i.then_inc(s_mixp, 1)

            def a_delta(n):
                pe.wait_ge(s_mix, n + 1)
                for f in range(4):
                    for m in range(HALVES):
                        i = mm(v((ps_a0, ps_a1)[f // 2], (f % 2 * 2 + m) * TOK, (1, TOK)),
                               c_("w2", f * 256 + m * P, (1, P)), mix[:, :])
                i.then_inc(s_delta, 1)

            def project(o, off, name, f, m0, m, width):
                for h in range(HALVES):
                    i = mm(v(o, off, (1, TOK), n=m), c_(name, h * width + m0, (1, m)),
                           v(xf, (f * 2 + h) * TOK, (1, TOK)), h == 0, h == 1)
                return i

            def a_round1(n):
                pe.wait_ge(s_xf, n + 1)
                for m in range(HALVES):
                    project(ps_a0, m * TOK, "wr", 0, m * P, P, 256)
                for m in range(HALVES):
                    project(ps_a0, 256 + m * TOK, "wk", 2, m * P, P, 256)
                project(ps_a1, 0, "gw1", 0, 0, 128, 128)
                project(ps_a1, TOK, "lowa", 1, 0, 96, 96)
                project(ps_a1, 2 * TOK, "lowk", 2, 0, 48, 48).then_inc(s_p1, 1)

            def a_round2(n):
                pe.wait_ge(s_c1, n + 1)
                for m in range(HALVES):
                    project(ps_a0, m * TOK, "wv", 3, m * P, P, 256)
                for m in range(HALVES):
                    mm(v(ps_a0, 256, (1, 256)), v(xf, (6 + m) * TOK, (1, TOK)), c_("wv", m * 256, (1, 256)),
                       m == 0, m == 1)
                for o, name in ((0, "dec2"), (256, "aaa2")):
                    for m in range(HALVES):
                        i = mm(v(ps_a1, o + m * TOK, (1, TOK)), c_(name, m * P, (1, P), n=96),
                               v(low_a, 0, (1, TOK), n=96))
                i.then_inc(s_p2, 1)

            def a_round3(n):
                pe.wait_ge(s_c2, n + 1)
                for m in range(HALVES):
                    mm(v(ps_a0, m * TOK, (1, TOK)), c_("ma2", m * P, (1, P), n=96), v(low_a, 0, (1, TOK), n=96))
                for m in range(HALVES):
                    mm(v(ps_a0, 256 + m * TOK, (1, TOK)), c_("mk2", m * P, (1, P), n=48), v(low_k, 0, (1, TOK), n=48))
                for m in range(HALVES):
                    mm(v(ps_a1, m * TOK, (1, TOK)), c_("kkk2", m * P, (1, P), n=48), v(low_k, 0, (1, TOK), n=48))
                mm(v(ps_a1, 256, (1, 256)), tgate[:, :], c_("gw2", 0, (1, 256))).then_inc(s_p3, 1)

            def a_head_sums(n, src, o, done):
                for m in range(HALVES):
                    i = mm(v(o, m * HH, (1, HH)), v(src, m * TOK, (1, TOK)), c_("headcol", 0, (1, HH)))
                i.then_inc(done, 1)

            def a_inverse(n):
                pe.wait_ge(s_inv, n + 1)
                te.transpose(v(ps_a1, 0, (1, TOK), n=H), inv_n[:, :], ident).then_inc(s_invtp, 1)

            def a_inverse_rows(n):
                pe.wait_ge(s_invt, n + 1)
                for m in range(HALVES):
                    i = mm(v(ps_a0, m * TOK, (1, TOK)), c_("headrow", m * P, (1, P), n=H), v(inv_nt, 0, (1, TOK), n=H))
                i.then_inc(s_invb, 1)

            def a_queries(n, p):
                pe.wait_ge(s_kkb, n + 1)
                for m in range(4):
                    for h in range(HALVES):
                        i = mm(v(ps_a0, m * TOK, (1, TOK)), c_("wq", h * 512 + m * P, (1, P)),
                               v(xnt[p], h * TOK, (1, TOK)), h == 0, h == 1)
                i.then_inc(s_q, 1)

            def a_scores(n):
                pe.wait_ge(s_qt, n + 1)
                pe.wait_ge(s_da, DVE_LINKS[0] * n + DVE_LINKS[0])
                for m in range(4):
                    i = mm(v((ps_a0, ps_a1)[m // 2], (m % 2) * 256, (1, 256)), v(q_t, m * TOK, (1, TOK)),
                           c_("kbd", 0, (1, 256)))
                i.then_inc(s_scp, 1)

            def b_picks(n):
                pe.wait_ge(s_sel, n + 1)
                need(pe, s_g, NCH * n)
                for m, src in enumerate((hif, lof, wsel)):
                    i = te.transpose(v(ps_s[0], m * TOK, (1, TOK), n=SEL), src[:, :], ident)
                i.then_inc(s_selp, 1)

            def c_down(n, q):
                if q == 0:
                    pe.wait_ge(s_xh, n + 1)
                if q >= 2 or not isinstance(n, int) or n > 0:
                    pe.wait_ge(s_gelu, 8 * n + q - 1)
                for e in range(4):
                    for h in range(HALVES):
                        i = mm(v(ps_h[q % 2], e * TOK, (1, TOK)), v(wdown, (h * ER + q * 4 + e) * P, (1, P)),
                               v(xh, h * TOK, (1, TOK)), h == 0, h == 1)
                i.then_inc(s_h, 1)

            def c_weights(n, k):
                pe.wait_ge(s_oh, NCH * n + k + 1)
                if k == 1:
                    pe.wait_ge(s_oatt, n + 1)
                if k >= 2:
                    pe.wait_ge(s_g, NCH * n + k - 1)
                for m in range(CH):
                    o = v(ps_s[k % 2], m * ER, (1, ER))
                    lhs = v(oh_a[k % 2], (m // 2) * 2 * P + m % 2, (2, P), n=SEL)
                    at = (m // 2) * 2 * ER + m % 2
                    mm(o, lhs, v(oh_1[k % 2], at, (2, ER), n=SEL), True, False)
                    i = mm(o, lhs, v(oh_2[k % 2], at, (2, ER), n=SEL), False, True)
                i.then_inc(s_s, 1)

            def c_y(n):
                pe.wait_ge(s_z, n + 1)
                need(pe, s_g, NCH * n)
                for h in range(HALVES):
                    for m in range(N):
                        i = mm(v(ps_s[1], h * P + m, (N, HH)), v(hist, (h * N + m) * TOK, (1, TOK)),
                               c_("headcol", 0, (1, HH)))
                i.then_inc(s_y, 1)

            def c_transpose(n):
                pe.wait_ge(s_yn, n + 1)
                for m in range(HALVES):
                    i = te.transpose(v(ps_s[1], 256 + m * TOK, (1, TOK)), v(yn, m * P, (1, P)), ident)
                i.then_inc(s_ytp, 1)

            def c_project(n):
                pe.wait_ge(s_yt, n + 1)
                for m in range(HALVES):
                    i = mm(v(ps_s[1], 0, (1, C)), v(yt, m * TOK, (1, TOK)), c_("wo", m * 256, (1, 256)), m == 0, m == 1)
                i.then_inc(s_o, 1)

            def c_up(n, e0, e1):
                if e0 == 0:
                    pe.wait_ge(s_g, NCH * n + NCH)
                    need(pe, s_out, n)
                for e in range(e0, e1):
                    i = mm(v(ps_f, 0, (1, C)), v(gh, e * TOK, (1, TOK)), v(wup, e * C, (1, C)), e == 0, e == ER - 1)
                if e1 == ER:
                    i.then_inc(s_up, 1)

            def body(t, par, a, b, c, f):
                nxt = 1 - par
                n = t + 1
                for j in range(J):
                    if b:
                        pe.wait_ge(s_tkk, J * t + j + 1)
                        mm(v(ps_u, 0, (1, SW)), c_("headones", 0, (1, P)), t_kk[:, :]).then_inc(s_u, 1)
                        if j == 29:
                            b_picks(t)
                    if a:
                        if j == 2:
                            a_transpose(n)
                        if j == 4:
                            a_mix(n)
                        if j == 5:
                            a_delta(n)
                        if j == 8:
                            a_round1(n)
                        if j == 10:
                            a_round2(n)
                        if j == 12:
                            a_round3(n)
                        if j == 14:
                            pe.wait_ge(s_sq, n + 1)
                            a_head_sums(n, kk_sq, ps_a0, s_ssp)
                        if j == 16:
                            a_inverse(n)
                        if j == 17:
                            a_inverse_rows(n)
                        if j == 19:
                            a_queries(n, nxt)
                        if j == 20:
                            pe.wait_ge(s_rkf, n + 1)
                            a_head_sums(n, rkf, ps_a1, s_bonus)
                        if j == 24:
                            a_scores(n)
                    if c:
                        if j == 0:
                            c_y(t - 1)
                        if j in (1, 2, 3, 4, 6, 7, 9, 10):
                            c_down(t - 1, (1, 2, 3, 4, 6, 7, 9, 10).index(j))
                        if j == 6:
                            c_transpose(t - 1)
                        if j == 7:
                            c_project(t - 1)
                        if j in (9, 10, 13, 14, 15, 17, 19, 21):
                            c_weights(t - 1, (9, 10, 13, 14, 15, 17, 19, 21).index(j))
                        if j >= 25:
                            c_up(t - 1, min(ER, 5 * (j - 25)), min(ER, 5 * (j - 24)))

            pe.wait_ge(s_par, 64)
            rounds(pe, body)


def pack(inputs):
    import numpy as np
    g = {k: np.asarray(a) for k, a in inputs.items()}
    p = "L0_attn_"
    z = np.zeros((P, NCONST), g[p + "x"].dtype)

    def put(name, a, r0=0, off=0):
        a = np.asarray(a)
        z[r0:r0 + a.shape[0], COL[name] + off:COL[name] + off + a.shape[1]] = a

    def halves(name, wt):
        for c in range(2):
            put(name, wt[c * P:(c + 1) * P], off=c * wt.shape[1])

    halves("w1", g[p + "time_maa_w1"].T)
    for f in range(4):
        put("w2", g[p + "time_maa_w2"][f].T, r0=32 * f, off=256 * f)
    halves("wr", g[p + "receptance"].T)
    halves("wk", g[p + "key_w"].T)
    halves("wv", g[p + "value"].T)
    halves("gw1", g[p + "gate_w1"].T)
    halves("lowa", np.concatenate([g[p + "time_decay_w1"], g[p + "time_aaa_w1"], g[p + "ma_w1"]], 0).T)
    pad = np.zeros((16, C), z.dtype)
    halves("lowk", np.concatenate([g[p + "time_kkk_w1"], pad, g[p + "mk_w1"]], 0).T)
    put("dec2", g[p + "time_decay_w2"].T, 0)
    put("aaa2", g[p + "time_aaa_w2"].T, 64)
    put("ma2", g[p + "ma_w2"].T, 80)
    put("kkk2", g[p + "time_kkk_w2"].T, 0)
    put("mk2", g[p + "mk_w2"].T, 32)
    put("gw2", g[p + "gate_w2"].T)
    halves("wq", g["L0_ffn_Wq"])
    for a in range(2):
        put("kbd", g["L0_ffn_K1"].T, 64 * a, 128 * a)
        put("kbd", g["L0_ffn_K2"].T, 64 * a + 32, 128 * a + 64)
    halves("wo", g[p + "output"].T)
    put("ident", np.eye(P))
    put("headones", np.kron(np.eye(HH), np.ones((N, N))))
    put("headcol", np.kron(np.eye(HH), np.ones((N, 1))))
    for c in range(2):
        put("headrow", np.kron(np.eye(HH), np.ones((1, N))), 8 * c, P * c)
    cols = lambda a: np.asarray(a).reshape(-1, P).T
    put("maax", cols(g[p + "time_maa_x"]))
    put("maa", cols(g[p + "time_maa"]))
    put("td", cols(g[p + "time_decay"]))
    put("ba", cols(g[p + "time_aaaaa"]))
    put("bma", cols(g[p + "time_misc_a"]))
    put("bmk", cols(g[p + "time_misc_k"]))
    put("fa", cols(g[p + "time_faaaa"]))
    put("bq", cols(g["L0_ffn_bq"]))
    put("lnw", np.broadcast_to(g[p + "ln_w"], (P, C)))
    put("lnb", np.broadcast_to(g[p + "ln_b"], (P, C)))
    put("iota_c", np.broadcast_to(np.arange(NCAND), (P, NCAND)))
    put("mhalf", np.full((P, 16), -0.5))
    def experts(w):
        return w[:NKEY * NKEY].reshape(NKEY, 2, ER, C).transpose(1, 0, 2, 3)
    up = np.ascontiguousarray(experts(g["L0_ffn_W_up"]).reshape(P, ER * C))
    down = experts(g["L0_ffn_W_down"]).reshape(P, ER, 2, P).transpose(3, 2, 1, 0)
    iota_e = np.broadcast_to(np.repeat(np.arange(P), 2), (P, 2 * P)).astype(z.dtype)
    return z, np.ascontiguousarray(down.reshape(P, 2 * ER * P)), up, iota_e


def kernel(**inputs):
    import numpy as _np
    import concourse.bacc as _bacc
    from concourse.bass_utils import run_bass_kernel_spmd as _run

    x = _np.asarray(inputs["L0_attn_x"])
    tiles = x.shape[1] // J
    xt = _np.ascontiguousarray(x.reshape(B, tiles, J, C).transpose(1, 0, 2, 3).reshape(tiles * TOK, C))
    params, down, up, iota_e = pack(inputs)
    arrays = {"in_x": xt, "in_params": params, "in_down": down, "in_up": up, "in_iota": iota_e}
    nc = _bacc.Bacc("TRN2", target_bir_lowering=False, num_devices=1)
    aps = [nc.dram_tensor(n, a.shape, F32, kind="ExternalInput").ap() for n, a in arrays.items()]
    vs = nc.dram_tensor("v_scratch", (C, TOK), F32, kind="Internal").ap()
    out = nc.dram_tensor("out_0", (tiles * TOK, C), F32, kind="ExternalOutput").ap()
    build(nc, *aps, vs, out, tiles)
    r = _run(nc, [arrays], core_ids=[0])
    y = _np.asarray(r.results[0]["out_0"])
    return y.reshape(tiles, B, J, C).transpose(1, 0, 2, 3).reshape(x.shape)
```

```python
from contextlib import ExitStack

import concourse.bass as bass
from concourse import mybir

P = 128
B = 4
C = 256
HALVES = 2
J = 32
TOK = B * J
H = 16
N = 16
HH = 8
FH = 8
NKEY = 64
TOPK = 10
RUNS = ((0, 1, 10, 0), (1, 1, 5, 10), (2, 1, 3, 15), (3, 2, 2, 18), (5, 5, 1, 22))
NCAND = sum(ni * nj for _, ni, nj, _ in RUNS)
SEL = FH * TOPK
RING = 8
ER = 32
CH = 16
NCH = TOK // CH
DVE_LINKS = (2, 6, 117, 8, 2)
WSCALE = 8192.0
NEG = -3.0e38
LN_EPS = 1e-5
GN_EPS = 0.00064

DOWN_AT = (0, 0, 0, 1, 1, 4, 5, 6, 7, 7, 8, 9, 11, 12, 12, 13)
WEIGHTS_AT = (15, 16, 17, 18, 19, 20, 21, 23)
ONE_HOTS_AT = (2, 7, 16, 17, 18, 19, 20, 22)
WEIGH_AT = (16, 17, 18, 19, 20, 21, 22, 24)
Y_AT = (2, 3, 4, 5)
KEYS_AT = (0, 3, 5, 6)
PAIRS_AT = (11, 13)
CODES_AT = (25, 26, 27, 28)
UP_AT = 25
UP_ROWS = (0, 5, 10, 15, 20, 25, 29, 32)

F32 = mybir.dt.float32
F16 = mybir.dt.float16
U32 = mybir.dt.uint32
I32 = mybir.dt.int32
ALU = mybir.AluOpType
ACT = mybir.ActivationFunctionType
AX = mybir.AxisListType.X

LAYOUT = [
    ("w1", 2 * 128), ("w2", 4 * 256), ("wr", 2 * 256), ("wk", 2 * 256), ("wv", 2 * 256), ("gw1", 2 * 128),
    ("lowa", 2 * 112), ("lowk", 2 * 112), ("low2", 256), ("lowk2", 256),
    ("gw2", 256), ("wq", 2 * 512), ("kbd", 256), ("wo", 2 * 256), ("ident", 128), ("headones", 128),
    ("headmean", 128), ("headcol", 8), ("headrow", 2 * 128), ("spread", 143),
    ("maax", 2), ("maa", 8), ("td", 2), ("ba", 2), ("bma", 2), ("bmk", 2), ("fa", 2), ("bq", 4), ("lnw", 2), ("lnb", 2),
    ("iota_c", NCAND + 1), ("mhalf", H),
]
COL = {}
_at = 0
for _n, _w in LAYOUT:
    COL[_n] = _at
    _at += _w
NCONST = _at


class Part:

    def __init__(self, tensor, at, width):
        self.tensor, self.at, self.width = tensor, at, width

    def __getitem__(self, key):
        return self.tensor[:, self.at:self.at + self.width]


def v(t, off, *dims, p0=0, n=P):
    if isinstance(t, Part):
        off, t = off + t.at, t.tensor
    a = t[p0:p0 + n, :]
    return bass.AP(a.tensor, a.offset + off, [list(a.ap[0])] + [list(d) for d in dims])


def build(nc, x, params, down, up, iota_e, vscratch, out, tiles):
    with ExitStack() as ctx:
        def sb(name, width, dt=F32, parts=P):
            return ctx.enter_context(nc.sbuf_tensor(name, [parts, width], dt))

        def sem(name):
            return ctx.enter_context(nc.semaphore(name))

        def bank(name):
            return ctx.enter_context(nc.psum_tensor(name, [P, 512], F32))

        ps_u = bank("ps_u")
        ps_a0, ps_a1 = bank("ps_a0"), bank("ps_a1")
        ps_h = [bank("ps_h0"), bank("ps_h1")]
        ps_s = [bank("ps_s0"), bank("ps_s1")]
        ps_f = bank("ps_f")

        cst = sb("cst", NCONST)
        wdown = sb("wdown", HALVES * ER * P)
        wup = sb("wup", ER * C)
        iota_e16 = sb("iota_e16", 256, F16)
        ntd = sb("ntd", 2)
        hba = sb("hba", 2)
        hbma = sb("hbma", 2)
        hbmk = sb("hbmk", 2)
        mhalf_b = sb("mhalf_b", 1)
        half_b = sb("half_b", 1)
        gn_eps = sb("gn_eps", 1)

        def c_(name, off, *dims, p0=0, n=P):
            return v(cst, COL[name] + off, *dims, p0=p0, n=n)

        def both(name, width):
            return [sb(f"{name}{i}", width) for i in range(2)]

        W2 = HALVES * TOK
        x_in = sb("x_in", C)
        stats = sb("stats", 6)
        meanvar = sb("meanvar", 2)
        vareps = sb("vareps", 1)
        rstd = sb("rstd", 1)
        xt = sb("xt", HALVES * B * (J + 1))
        xnt = both("xnt", W2)
        xh = sb("xh", W2)
        xx = sb("xx", W2)
        tgate = Part(xx, 0, TOK)
        low_a = Part(xx, TOK, TOK)
        low_k = mix = sb("low_k", TOK)
        xxx = sb("xxx", W2)
        kk_sq = rkf = xxx
        xf = sb("xf", 4 * W2)
        r_t = both("r_t", W2)
        k_t = sb("k_t", W2)
        bv = both("bv", W2)
        gate = both("gate", W2)
        absz = sb("absz", W2)
        wm = expwm = absz
        reluz = sb("reluz", W2)
        spl = reluz
        not_ma = sb("not_ma", W2)
        mk_t = sb("mk_t", W2)
        q_t = Part(xf, 512, 4 * TOK)
        ss = sb("ss", H)
        inv_n = sb("inv_n", H)
        inv_t = Part(low_k, 0, TOK)
        kk = both("kk", W2)
        b_t = both("b_t", W2)
        expw = both("expw", W2)
        k_fin = sb("k_fin", W2)
        scores = sb("scores", FH * 2 * NKEY)
        scores2 = sb("scores2", 4 * NKEY)

        SW = HALVES * B * N
        JH = J // 2
        ring = sb("ring", RING * SW)
        zr = sb("zr", J * SW)
        vk = [sb(f"vk{i}", HALVES * N * B * JH) for i in range(2)]
        t_kk = sb("t_kk", SW)
        t_dvk = sb("t_dvk", SW)

        STATE = [(B * N, HALVES), (N, B), (1, N)]

        def state_after(step):
            return v(ring, step % RING * SW, *STATE)

        topv = sb("topv", 16 * 16)
        topi = sb("topi", 16 * 16, U32)
        topif = Part(scores, 0, 256)
        hi_f = Part(scores, 256, FH * 16)
        cand = sb("cand", FH * NCAND)
        candi = sb("candi", FH * NCAND)
        cand2 = sb("cand2", 4 * NCAND)
        vals = sb("vals", FH * 16)
        pos = sb("pos", FH * 16, U32)
        posf = sb("posf", FH * 16)
        eqp = xf
        sel = sb("sel", SEL)
        sel_i = sb("sel_i", SEL, I32)
        sel_lo = sb("sel_lo", SEL, I32)
        sel_hi = sb("sel_hi", SEL, I32)
        lof = sel
        hif = sb("hif", SEL)
        dif = sb("dif", SEL)
        ex = sb("ex", SEL)
        sume = sb("sume", FH)
        rsum = sb("rsum", FH)
        wsel = sb("wsel", SEL)
        hi_t = sb("hi_t", TOK, F16, SEL)
        lo_t = sb("lo_t", TOK, F16, SEL)
        w1_t = sb("w1_t", TOK, F16, SEL)
        w2_t = sb("w2_t", TOK, F16, SEL)
        oh_a = [sb(f"oh_a{i}", CH * P, F16, SEL) for i in range(2)]
        oh_e = sb("oh_e", CH * ER, F16, SEL)
        oh_1 = [sb(f"oh_1{i}", CH * ER, F16, SEL) for i in range(2)]
        oh_2 = [sb(f"oh_2{i}", CH * ER, F16, SEL) for i in range(2)]
        gh = sb("gh", ER * TOK)

        yc = sb("yc", W2)
        ysq = sb("ysq", W2)
        yve = sb("yve", H)
        yrs = sb("yrs", H)
        yrs_t = Part(ysq, 0, TOK)
        o_att = sb("o_att", C)
        sg_f = sb("sg_f", C)
        y_out = sb("y_out", C)

        s_par = sem("s_par")
        s_pre = sem("s_pre")
        s_x = sem("s_x")
        s_xr = sem("s_xr")
        s_vare = sem("s_vare")
        s_rstd = sem("s_rstd")
        s_xn = sem("s_xn")
        s_xtp = sem("s_xtp")
        s_xt = sem("s_xt")
        s_xh = sem("s_xh")
        s_xxx = sem("s_xxx")
        s_mixp = sem("s_mixp")
        s_mix = sem("s_mix")
        s_delta = sem("s_delta")
        s_xf = sem("s_xf")
        s_gated = sem("s_gated")
        s_q = sem("s_q")
        s_qt = sem("s_qt")
        s_scp = sem("s_scp")
        s_scores = sem("s_scores")
        s_p1 = sem("s_p1")
        s_c1 = sem("s_c1")
        s_p2 = sem("s_p2")
        s_vt = sem("s_vt")
        s_c2 = sem("s_c2")
        s_p3 = sem("s_p3")
        s_c3 = sem("s_c3")
        s_kkraw = sem("s_kkraw")
        s_sq = sem("s_sq")
        s_ssp = sem("s_ssp")
        s_ss = sem("s_ss")
        s_inv = sem("s_inv")
        s_ln1 = sem("s_ln1")
        s_spl = sem("s_spl")
        s_expw = sem("s_expw")
        s_wm = sem("s_wm")
        s_expwm = sem("s_expwm")
        s_kkb = sem("s_kkb")
        s_kfin = sem("s_kfin")
        s_rkf = sem("s_rkf")
        s_bonus = sem("s_bonus")
        s_vdram = sem("s_vdram")
        s_vb = [sem("s_vb0"), sem("s_vb1")]
        s_vk = sem("s_vk")
        s_tkk = sem("s_tkk")
        s_u = sem("s_u")
        s_ub = sem("s_ub")
        s_dvk = sem("s_dvk")
        s_state = sem("s_state")
        s_z = sem("s_z")
        s_h = sem("s_h")
        s_gelu = sem("s_gelu")
        s_vals = sem("s_vals")
        s_ex = sem("s_ex")
        s_sel = sem("s_sel")
        s_selp = sem("s_selp")
        s_selc = sem("s_selc")
        s_w2 = sem("s_w2")
        s_oh = sem("s_oh")
        s_s = sem("s_s")
        s_g = sem("s_g")
        s_up = sem("s_up")
        s_y = sem("s_y")
        s_ys = sem("s_ys")
        s_ymp = sem("s_ymp")
        s_yvp = sem("s_yvp")
        s_yr = sem("s_yr")
        s_yl = sem("s_yl")
        s_yc = sem("s_yc")
        s_yrtp = sem("s_yrtp")
        s_yrt = sem("s_yrt")
        s_yrb = sem("s_yrb")
        s_invtp = sem("s_invtp")
        s_invt = sem("s_invt")
        s_invb = sem("s_invb")
        s_ysq = sem("s_ysq")
        s_yve = sem("s_yve")
        s_yrs = sem("s_yrs")
        s_yn = sem("s_yn")
        s_o = sem("s_o")
        s_oatt = sem("s_oatt")
        s_thf = sem("s_thf")
        s_out = sem("s_out")
        s_stored = sem("s_stored")
        s_tick = sem("s_tick")
        s_ds = sem("s_ds")
        s_da = sem("s_da")
        s_db = sem("s_db")
        s_dc = sem("s_dc")
        s_df = sem("s_df")
        s_act = sem("s_act")
        s_pd = sem("s_pd")

        def need(engine, semaphore, count):
            if not (isinstance(count, int) and count <= 0):
                engine.wait_ge(semaphore, count)

        class Chain:

            def __init__(self, engine, semaphore, per_tile):
                self.engine, self.semaphore, self.per_tile = engine, semaphore, per_tile

            def start(self, t):
                self.base, self.count = t * self.per_tile, 0

            def inc(self, instruction):
                self.count += 1
                instruction.then_inc(self.semaphore, 1)

            def wait(self):
                self.engine.wait_ge(self.semaphore, self.base + self.count)

            def link(self, instruction):
                self.inc(instruction)
                self.wait()

            def settle(self):
                self.wait()
                self.engine.sem_inc(s_tick, 1)

            def end(self):
                assert self.count == self.per_tile, (self.semaphore, self.count)

        def rounds(engine, body):
            def at(t):
                body(t, t % 2, t + 1 in range(tiles), t in range(tiles), t - 1 in range(tiles), t - 2 in range(tiles))

            for t in (-1, 0, 1):
                at(t)
            with engine.Fori(2, tiles - 2, 2) as t:
                body(t, 0, True, True, True, True)
                body(t + 1, 1, True, True, True, True)
            for t in range(tiles - 2, tiles + 2):
                at(t)

        block = ctx.enter_context(nc.Block())

        @block.sync
        def _(sp):
            def tile_of(dram, t):
                return bass.AP(dram.tensor, t * (TOK * C), [[C, TOK], [1, C]])

            HALF = HALVES * N * B * JH

            def broadcast_v(t, i):
                for h in range(HH):
                    sp.dma_start(v(vk[i], 0, (1, HALF), p0=h * N, n=N),
                                 bass.AP(vscratch.tensor, (h * 2 + i) * HALF, [[0, N], [1, HALF]])
                                 ).then_inc(s_vb[i], 16)

            def body(t, par, a, b, c, f):
                if b:
                    need(sp, s_dvk, J * t)
                    broadcast_v(t, 1)
                if f:
                    sp.wait_ge(s_out, t - 1)
                    sp.dma_start(tile_of(out, t - 2), y_out[:, :]).then_inc(s_stored, 16)
                if c:
                    need(sp, s_stored, 16 * (t - 1))
                    sp.dma_start(y_out[:, :], tile_of(x, t - 1)).then_inc(s_xr, 16)
                if a:
                    if not isinstance(t, int) or t + 2 < tiles:
                        sp.wait_ge(s_xtp, t + 2)
                        sp.dma_start(x_in[:, :], tile_of(x, t + 2)).then_inc(s_x, 16)
                    if b:
                        sp.wait_ge(s_vb[1], 16 * HH * t + 16 * HH)
                    sp.wait_ge(s_vt, t + 2)
                    for i in range(2):
                        for m in range(HALVES):
                            sp.dma_start(
                                bass.AP(vscratch.tensor, i * HALF + m * (N * B * JH),
                                        [[2 * HALF, HH], [B * JH, N], [JH, B], [1, JH]]),
                                v(bv[1 - par], m * TOK + i * JH, (J, B), (1, JH))).then_inc(s_vdram, 16)
                    sp.wait_ge(s_vdram, 64 * t + 128)
                    sp.sem_inc(s_tick, 1)
                    need(sp, s_dvk, J * t + JH)
                    broadcast_v(t + 1, 0)

            sp.dma_start(cst[:, :], params).then_inc(s_par, 16)
            sp.dma_start(v(gh, 0, (1, 256)), iota_e).then_inc(s_par, 16)
            sp.dma_start(x_in[:, :], tile_of(x, 0)).then_inc(s_x, 16)
            sp.dma_start(wdown[:, :], down).then_inc(s_par, 16)
            sp.dma_start(wup[:, :], up).then_inc(s_par, 16)
            rounds(sp, body)
            sp.wait_ge(s_stored, 16 * tiles)

        @block.gpsimd
        def _(pool):
            gp = nc.gpsimd

            def layer_norm_root(n):
                pool.wait_ge(s_vare, n + 1)
                gp.tensor_tensor(rstd[:, :], vareps[:, :], c_("mhalf", 0, (1, 1)), ALU.pow).then_inc(s_rstd, 1)

            def body(t, par, a, b, c, f):
                def times_k(i, piece):
                    m, v0 = piece // 4, piece % 4 * 4
                    o = v(vk[i], (m * N + v0) * B * JH, (B * JH, 4), (JH, B), (1, JH))
                    gp.tensor_tensor(o, o, v(k_fin, m * TOK + i * JH, (0, 4), (J, B), (1, JH)),
                                     ALU.mult).then_inc(s_vk, 1)

                def times_r(step, p):
                    q = step // 4
                    for m in range(HALVES):
                        i = gp.tensor_tensor(v(zr, m * N * TOK + 4 * q, (J, B), (TOK, N), (1, 4)),
                                             v(ring, q % 2 * 4 * SW + m * B * N, (N, B), (1, N), (SW, 4)),
                                             v(r_t[p], m * TOK + 4 * q, (J, B), (0, N), (1, 4)), ALU.mult)
                    i.then_inc(s_z, 1)

                for j in range(J):
                    if b:
                        need(pool, s_state, J * t + j)
                        if j == 0:
                            pool.wait_ge(s_expw, t + 1)
                        gp.tensor_tensor(v(t_dvk, 0, *STATE), state_after(j - 1),
                                         v(expw[par], j, (TOK, HALVES), (J, B), (0, N)), ALU.mult).then_inc(s_pd, 1)
                        if j % JH == 0:
                            pool.wait_ge(s_vk, 16 * t + 8 + 8 * (j // JH))
                        pool.wait_ge(s_pd, J * t + j + 1)
                        gp.tensor_tensor(v(t_dvk, 0, *STATE), v(t_dvk, 0, *STATE),
                                         v(vk[j // JH], j % JH, (N * B * JH, HALVES), (JH, B), (B * JH, N)),
                                         ALU.add).then_inc(s_dvk, 1)
                        if j in (6, 8, 12, 16, 20, 24, 28):
                            if j == 6:
                                need(pool, s_y, t)
                            times_r(j // 4 * 4 - 1, par)
                    if c and j == 0:
                        pool.wait_ge(s_state, J * t)
                        times_r(J - 1, 1 - par)
                    if j == 30 and (not isinstance(t, int) or t + 2 < tiles):
                        layer_norm_root(t + 2)
                    if b and 2 <= j < 10:
                        if j == 2:
                            pool.wait_ge(s_vb[1], 16 * HH * t + 16 * HH)
                            pool.wait_ge(s_kfin, t + 1)
                        times_k(1, j - 2)
                    if c and j in (9, 10, 11):
                        if j == 9:
                            pool.wait_ge(s_yve, t)
                        at, n = {9: (0, 5), 10: (5, 5), 11: (10, 6)}[j]
                        gp.tensor_tensor(v(yrs, at, (1, n)), v(yve, at, (1, n)), c_("mhalf", 0, (1, n)),
                                         ALU.pow).then_inc(s_yrs, 1)
                    if c and j == 15:
                        pool.wait_ge(s_yl, t)
                        gp.tensor_tensor(yc[:, :], yc[:, :], bv[1 - par][:, :], ALU.add).then_inc(s_gated, 1)
                        pool.wait_ge(s_gated, t)
                        gp.tensor_tensor(yc[:, :], yc[:, :], gate[1 - par][:, :], ALU.mult).then_inc(s_yn, 1)
                    if a and j == 18:
                        pool.wait_ge(s_c3, t + 2)
                        gp.tensor_tensor(kk[1 - par][:, :], k_t[:, :], kk[1 - par][:, :], ALU.add).then_inc(s_kkraw, 1)
                    if a and j == 20:
                        pool.wait_ge(s_ss, t + 2)
                        gp.tensor_tensor(inv_n[:, :], ss[:, :], c_("mhalf", 0, (1, H)), ALU.pow).then_inc(s_inv, 1)
                    if a and 24 <= j < 32:
                        if j == 24:
                            pool.wait_ge(s_vb[0], 16 * HH * t + 32 * HH)
                            pool.wait_ge(s_kfin, t + 2)
                        times_k(0, j - 24)

            pool.wait_ge(s_par, 64)
            layer_norm_root(0)
            rounds(pool, body)

        @block.scalar
        def _(act):
            sc = nc.scalar
            chain = Chain(act, s_act, 4)

            def body(t, par, a, b, c, f):
                nxt = 1 - par

                for j in range(J):
                    if f and j == 0:
                        act.wait_ge(s_up, t - 1)
                        sc.activation(sg_f[:, :], v(ps_f, 0, (1, C)), ACT.Tanh, scale=0.5 / WSCALE).then_inc(s_thf, 1)
                    for q in [q for q in range(8) if c and DOWN_AT[2 * q + 1] == j]:
                        if q == 0:
                            need(act, s_up, t - 1)
                        act.wait_ge(s_h, 8 * t + (q - 7))
                        sc.activation(v(gh, q * 512, (1, 512)), ps_h[q % 2][:, :], ACT.Gelu).then_inc(s_gelu, 1)
                    if a and j == 2:
                        chain.start(t + 1)
                        act.wait_ge(s_xtp, t + 2)
                        chain.link(sc.copy(v(xt, 0, (B * (J + 1), HALVES), (J + 1, B), (1, 1)),
                                           v(xt, J, (B * (J + 1), HALVES), (J + 1, B), (1, 1))))
                        sc.copy(v(xt, 1, (B * (J + 1), HALVES), (J + 1, B), (1, J)),
                                v(ps_a0, 0, (TOK, HALVES), (J, B), (1, J)))
                        need(act, s_xh, t)
                        sc.copy(xnt[nxt][:, :], v(ps_a0, 0, (1, W2))).then_inc(s_xt, 1)
                    if a and j == 5:
                        act.wait_ge(s_mixp, t + 2)
                        sc.activation(mix[:, :], v(ps_a1, 0, (1, TOK)), ACT.Tanh).then_inc(s_mix, 1)
                    if c and j == 5:
                        act.wait_ge(s_y, t)
                        need(act, s_o, t - 1)
                        sc.copy(yc[:, :], v(ps_f, 0, (1, W2))).then_inc(s_ys, 1)
                    if c and j == 7:
                        act.wait_ge(s_yc, t)
                        sc.activation(ysq[:, :], yc[:, :], ACT.Square).then_inc(s_ysq, 1)
                    if c and j == 8:
                        act.wait_ge(s_yvp, t)
                        sc.activation(yve[:, :], v(ps_f, 0, (1, H)), ACT.Identity, bias=gn_eps[:, :],
                                      scale=1.0 / N).then_inc(s_yve, 1)
                    if c and j == 12:
                        act.wait_ge(s_yrtp, t)
                        sc.copy(v(yrs_t, 0, (1, TOK), n=H), v(ps_f, 0, (1, TOK), n=H)).then_inc(s_yrt, 1)
                    if a and j == 11:
                        act.wait_ge(s_p1, t + 2)
                        need(act, s_z, 8 * t)
                        sc.copy(r_t[nxt][:, :], v(ps_a0, 0, (1, 256)))
                        sc.copy(k_t[:, :], v(ps_a0, 256, (1, 256)))
                        sc.activation(tgate[:, :], v(ps_a1, 0, (1, TOK)), ACT.Tanh)
                        sc.activation(v(low_a, 0, (1, TOK), n=64), v(ps_a1, TOK, (1, TOK), n=64), ACT.Tanh)
                        sc.copy(v(low_a, 0, (1, TOK), p0=64, n=48), v(ps_a1, TOK, (1, TOK), p0=64, n=48))
                        sc.activation(v(low_k, 0, (1, TOK), n=32), v(ps_a1, 2 * TOK, (1, TOK), n=32), ACT.Tanh)
                        sc.copy(v(low_k, 0, (1, TOK), p0=96, n=16),
                                v(ps_a1, 2 * TOK, (1, TOK), p0=96, n=16)).then_inc(s_c1, 1)
                    if c and j == 14:
                        act.wait_ge(s_yr, t)
                        for m in range(HALVES):
                            i = sc.activation(v(yc, m * TOK, (1, TOK)), v(yc, m * TOK, (1, TOK)), ACT.Identity,
                                              bias=c_("lnb", m, (1, 1)), scale=c_("lnw", m, (1, 1)))
                        i.then_inc(s_yl, 1)
                    if a and j == 14:
                        act.wait_ge(s_p2, t + 2)
                        for m in range(HALVES):
                            sc.activation(v(absz, m * TOK, (1, TOK)), v(ps_a1, m * TOK, (1, TOK)), ACT.Abs,
                                          bias=c_("td", m, (1, 1)))
                            sc.activation(v(reluz, m * TOK, (1, TOK)), v(ps_a1, m * TOK, (1, TOK)), ACT.Relu,
                                          bias=v(ntd, m, (1, 1)), scale=-1.0)
                        for m in range(HALVES):
                            i = sc.activation(v(b_t[nxt], m * TOK, (1, TOK)), v(ps_a1, 256 + m * TOK, (1, TOK)),
                                              ACT.Tanh, bias=v(hba, m, (1, 1)), scale=0.5)
                        chain.link(i)
                        sc.activation(b_t[nxt][:, :], b_t[nxt][:, :], ACT.Identity, bias=half_b[:, :],
                                      scale=-0.5).then_inc(s_c2, 1)
                    if a and j == 16:
                        need(act, s_yn, t)
                        sc.copy(bv[nxt][:, :], v(ps_a0, 0, (1, 256))).then_inc(s_vt, 1)
                    if c and j == 16:
                        act.wait_ge(s_o, t)
                        need(act, s_out, t - 1)
                        sc.copy(o_att[:, :], v(ps_f, 256, (1, C))).then_inc(s_oatt, 1)
                    if a and j == 17:
                        act.wait_ge(s_p3, t + 2)
                        for m in range(HALVES):
                            sc.activation(v(not_ma, m * TOK, (1, TOK)), v(ps_a0, m * TOK, (1, TOK)), ACT.Tanh,
                                          bias=v(hbma, m, (1, 1)), scale=0.5)
                            i = sc.activation(v(mk_t, m * TOK, (1, TOK)), v(ps_a0, 256 + m * TOK, (1, TOK)), ACT.Tanh,
                                              bias=v(hbmk, m, (1, 1)), scale=0.5)
                        chain.inc(i)
                        sc.copy(kk[nxt][:, :], v(ps_a1, 0, (1, 256)))
                        chain.wait()
                        sc.activation(not_ma[:, :], not_ma[:, :], ACT.Identity, bias=half_b[:, :], scale=-0.5)
                        sc.activation(mk_t[:, :], mk_t[:, :], ACT.Identity, bias=half_b[:, :], scale=0.5)
                        sc.copy(gate[nxt][:, :], v(ps_a1, 256, (1, 256))).then_inc(s_c3, 1)
                    if b and j == 15:
                        need(act, s_h, 8 * t)
                        sc.copy(xh[:, :], xnt[par][:, :]).then_inc(s_xh, 1)
                    if b and j == 16:
                        act.wait_ge(s_vals, t + 1)
                        sc.activation(ex[:, :], dif[:, :], ACT.Exp).then_inc(s_ex, 1)
                    if a and j == 18:
                        act.wait_ge(s_kkraw, t + 2)
                        sc.activation(kk_sq[:, :], kk[nxt][:, :], ACT.Square).then_inc(s_sq, 1)
                        chain.link(sc.activation(absz[:, :], absz[:, :], ACT.Exp, scale=-1.0))
                        sc.activation(absz[:, :], absz[:, :], ACT.Ln, bias=1.0).then_inc(s_ln1, 1)
                    if a and j == 20:
                        act.wait_ge(s_q, t + 2)
                        for m in range(4):
                            i = sc.activation(v(q_t, m * TOK, (1, TOK)), v(ps_a0, m * TOK, (1, TOK)), ACT.Identity,
                                              bias=c_("bq", m, (1, 1)))
                        i.then_inc(s_qt, 1)
                    if a and j == 21:
                        act.wait_ge(s_invtp, t + 2)
                        sc.copy(v(inv_t, 0, (1, TOK), n=H), v(ps_a1, TOK, (1, TOK), n=H)).then_inc(s_invt, 1)
                    if a and j == 21:
                        act.wait_ge(s_spl, t + 2)
                        need(act, s_dvk, J * t)
                        sc.activation(expw[nxt][:, :], spl[:, :], ACT.Exp, bias=mhalf_b[:, :],
                                      scale=-1.0).then_inc(s_expw, 1)
                        act.wait_ge(s_wm, t + 2)
                        sc.activation(expwm[:, :], wm[:, :], ACT.Exp, scale=-1.0).then_inc(s_expwm, 1)
                    if a and j in (22, 23):
                        act.wait_ge(s_scp, 2 * t + 3 + (j - 22))
                        sc.copy(v(scores, 512 * (j - 22), (1, 512)), ps_a0[:, :]).then_inc(s_scores, 1)
                    if b and j == 31:
                        act.wait_ge(s_selp, t + 1)
                        need(act, s_oh, NCH * t)
                        sc.copy(hi_t[:, :], v(ps_s[0], 0, (1, TOK), n=SEL))
                        sc.copy(lo_t[:, :], v(ps_s[0], TOK, (1, TOK), n=SEL))
                        sc.activation(w1_t[:, :], v(ps_s[0], 2 * TOK, (1, TOK), n=SEL), ACT.Copy,
                                      scale=WSCALE).then_inc(s_selc, 1)

            act.wait_ge(s_par, 64)
            act.wait_ge(s_pre, 1)
            rounds(act, body)

        @block.vector
        def _(dve):
            ve = nc.vector
            ve.memset(xt[:, :], 0.0)
            ve.memset(ring[:, :], 0.0)
            ve.memset(mhalf_b[:, :], -0.5)
            ve.memset(half_b[:, :], 0.5)
            ve.memset(gn_eps[:, :], GN_EPS)
            dve.wait_ge(s_par, 64)
            ve.tensor_scalar(ntd[:, :], c_("td", 0, (1, 2)), -1.0, None, ALU.mult)
            ve.tensor_scalar(hba[:, :], c_("ba", 0, (1, 2)), 0.5, None, ALU.mult)
            ve.tensor_scalar(hbma[:, :], c_("bma", 0, (1, 2)), 0.5, None, ALU.mult)
            ve.tensor_scalar(hbmk[:, :], c_("bmk", 0, (1, 2)), 0.5, None, ALU.mult)
            ve.tensor_copy(iota_e16[:, :], v(gh, 0, (1, 256))).then_inc(s_pre, 1)
            dve.wait_ge(s_pre, 1)
            cs, ca, cb, cc, cf = (Chain(dve, s, n) for s, n in zip((s_ds, s_da, s_db, s_dc, s_df), DVE_LINKS))

            def a_stats(n):
                cs.start(n)
                dve.wait_ge(s_x, 16 * n + 16)
                cs.inc(ve.bn_stats(stats[:, :], x_in[:, :]))
                cs.settle()
                cs.link(ve.bn_aggr(meanvar[:, :], stats[:, :]))
                ve.tensor_scalar(vareps[:, :], v(meanvar, 1, (1, 1)), LN_EPS, None, ALU.add).then_inc(s_vare, 1)

            def a_normalize(n):
                dve.wait_ge(s_rstd, n + 1)
                ve.tensor_scalar(x_in[:, :], x_in[:, :], v(meanvar, 0, (1, 1)), rstd[:, :],
                                 ALU.subtract, ALU.mult).then_inc(s_xn, 1)

            def a_shift(n, p):
                dve.wait_ge(s_xt, n + 1)
                ca.link(ve.tensor_tensor(v(xx, 0, (TOK, HALVES), (J, B), (1, J)),
                                         v(xt, 0, (B * (J + 1), HALVES), (J + 1, B), (1, J)),
                                         v(xt, 1, (B * (J + 1), HALVES), (J + 1, B), (1, J)), ALU.subtract))
                for m in range(HALVES):
                    i = ve.scalar_tensor_tensor(v(xxx, m * TOK, (1, TOK)), v(xx, m * TOK, (1, TOK)),
                                                c_("maax", m, (1, 1)), v(xnt[p], m * TOK, (1, TOK)),
                                                ALU.mult, ALU.add)
                i.then_inc(s_xxx, 1)

            def a_mixed(f, m):
                i = ve.scalar_tensor_tensor(
                    v(xf, (f * 2 + m) * TOK, (1, TOK)),
                    v((ps_a0, ps_a1)[f // 2], (f % 2 * 2 + m) * TOK, (1, TOK)),
                    c_("maa", f * 2 + m, (1, 1)), v(xx, m * TOK, (1, TOK)), ALU.add, ALU.mult)
                if (f, m) == (3, 1):
                    ca.inc(i)

            def a_mixed_add(n, p):
                ca.wait()
                ve.tensor_tensor(v(xf, 0, (256, 4), (1, 256)), v(xf, 0, (256, 4), (1, 256)),
                                 v(xnt[p], 0, (0, 4), (1, 256)), ALU.add).then_inc(s_xf, 1)

            def a_kmul(n, p):
                dve.wait_ge(s_c3, n + 1)
                need(dve, s_vk, 16 * n)
                ca.link(ve.tensor_tensor(k_fin[:, :], b_t[p][:, :], not_ma[:, :], ALU.mult))
                ca.inc(ve.scalar_tensor_tensor(k_fin[:, :], k_fin[:, :], -1.0, k_t[:, :], ALU.add, ALU.mult))

            def a_norm(n):
                dve.wait_ge(s_ssp, n + 1)
                ve.tensor_scalar(ss[:, :], v(ps_a1, 0, (1, H)), 1e-24, None, ALU.max).then_inc(s_ss, 1)

            def a_decay(n):
                dve.wait_ge(s_ln1, n + 1)
                ve.tensor_tensor(spl[:, :], reluz[:, :], absz[:, :], ALU.add).then_inc(s_spl, 1)
                dve.wait_ge(s_spl, n + 1)
                ve.scalar_tensor_tensor(wm[:, :], spl[:, :], 0.5, mk_t[:, :], ALU.add, ALU.mult).then_inc(s_wm, 1)

            def a_kk_b(n, p):
                dve.wait_ge(s_invb, n + 1)
                ca.link(ve.tensor_tensor(kk[p][:, :], kk[p][:, :], v(ps_a1, 256, (1, W2)), ALU.mult))
                ve.scalar_tensor_tensor(b_t[p][:, :], b_t[p][:, :], -1.0, kk[p][:, :],
                                        ALU.add, ALU.mult).then_inc(s_kkb, 1)

            def a_kfin(n, p):
                dve.wait_ge(s_expwm, n + 1)
                ca.wait()
                ve.scalar_tensor_tensor(k_fin[:, :], k_fin[:, :], -1.0, expwm[:, :],
                                        ALU.mult, ALU.mult).then_inc(s_kfin, 1)
                dve.wait_ge(s_kfin, n + 1)
                for m in range(HALVES):
                    i = ve.scalar_tensor_tensor(v(rkf, m * TOK, (1, TOK)), v(r_t[p], m * TOK, (1, TOK)),
                                                c_("fa", m, (1, 1)), v(k_fin, m * TOK, (1, TOK)), ALU.mult, ALU.mult)
                i.then_inc(s_rkf, 1)

            def a_bonus(n, p):
                dve.wait_ge(s_bonus, n + 1)
                dve.wait_ge(s_vdram, 64 * n + 64)
                ca.inc(ve.tensor_tensor(bv[p][:, :], bv[p][:, :], v(ps_a1, 0, (1, W2)), ALU.mult))

            def key_rows(q):
                return four_rows(q, NKEY, scores, topv, topi, scores2)

            def pair_rows(q):
                return four_rows(q, NCAND, cand, vals, pos, cand2)

            def four_rows(q, width, keys, top, at, rest):
                return [(v(keys, g * width, (1, width)), v(top, g * 16, (1, 8)), v(at, g * 16, (1, 8)),
                         v(rest, g % 4 * width, (1, width)), v(top, g * 16 + 8, (1, 8)), v(at, g * 16 + 8, (1, 8)))
                        for g in range(4 * q, 4 * q + 4)]

            def first_eight(rows):
                for keys, first, _, _, _, _ in rows:
                    cb.inc(ve.max(first, keys))

            def strike_out(rows):
                cb.settle()
                for keys, first, _, rest, _, _ in rows:
                    cb.inc(ve.match_replace(rest, first, keys, NEG))
                for keys, first, first_at, _, _, _ in rows:
                    ve.max_index(first_at, first, keys)

            def next_eight(rows):
                cb.settle()
                for _, _, _, rest, second, _ in rows:
                    cb.inc(ve.max(second, rest))

            def next_places(rows):
                cb.settle()
                for _, _, _, rest, second, second_at in rows:
                    cb.inc(ve.max_index(second_at, second, rest))

            def indices_as_floats():
                cb.wait()
                cb.inc(ve.tensor_copy(topif[:, :], topi[:, :]))

            def high_parts():
                cb.wait()
                cb.inc(ve.tensor_scalar(v(hi_f, 0, (16, FH), (1, 16)), v(topif, 16, (32, FH), (1, 16)), 31.5,
                                        2016.0, ALU.is_gt, ALU.mult))
                ve.tensor_scalar(v(topif, 0, (32, FH), (1, 16)), v(topif, 0, (32, FH), (1, 16)), 32.0,
                                 None, ALU.mult)

            def second_keys():
                cb.wait()
                cb.inc(ve.tensor_tensor(v(topif, 16, (32, FH), (1, 16)), v(topif, 16, (32, FH), (1, 16)),
                                        v(hi_f, 0, (16, FH), (1, 16)), ALU.add))

            def pair_up(dst, src, runs):
                for i0, ni, nj, at in runs:
                    i = ve.tensor_tensor(v(dst, at, (NCAND, FH), (nj, ni), (1, nj)),
                                         v(src, i0, (32, FH), (1, ni), (0, nj)),
                                         v(src, 16, (32, FH), (0, ni), (1, nj)), ALU.add)
                return i

            def differences():
                cb.wait()
                ve.tensor_tensor(v(dif, 0, (TOPK, FH), (1, TOPK)), v(vals, 0, (16, FH), (1, TOPK)),
                                 v(vals, 0, (16, FH), (0, TOPK)), ALU.subtract).then_inc(s_vals, 1)
                cb.inc(ve.tensor_copy(posf[:, :], pos[:, :]))

            grid = v(eqp, 0, (TOPK * NCAND, 2), (NCAND, TOPK), (1, NCAND))

            def codes_match(h):
                cb.wait()
                cb.inc(ve.tensor_tensor(grid, v(posf, 16 * h, (16, 2), (1, TOPK), (0, NCAND)),
                                        c_("iota_c", 0, (0, 2), (0, TOPK), (1, NCAND)), ALU.is_equal))

            def codes_pick(h):
                cb.wait()
                cb.inc(ve.tensor_tensor(grid, grid, v(candi, h * NCAND, (NCAND, 2), (0, TOPK), (1, NCAND)), ALU.mult))

            def codes_sum(h):
                cb.wait()
                cb.inc(ve.tensor_reduce(v(sel, h * TOPK, (TOPK, 2), (1, TOPK)), grid, AX, ALU.add))

            def coordinates(n):
                cb.wait()
                cb.link(ve.tensor_copy(sel_i[:, :], sel[:, :]))
                ve.tensor_scalar(sel_lo[:, :], sel_i[:, :], 31, None, ALU.bitwise_and)
                cb.link(ve.tensor_scalar(sel_hi[:, :], sel_i[:, :], 5, None, ALU.logical_shift_right))
                ve.tensor_copy(lof[:, :], sel_lo[:, :])
                ve.tensor_copy(hif[:, :], sel_hi[:, :])

            def softmax(n):
                dve.wait_ge(s_ex, n + 1)
                cb.link(ve.tensor_reduce(sume[:, :], v(ex, 0, (TOPK, FH), (1, TOPK)), AX, ALU.add))
                cb.link(ve.reciprocal(rsum[:, :], sume[:, :]))
                ve.tensor_tensor(v(wsel, 0, (TOPK, FH), (1, TOPK)), v(ex, 0, (TOPK, FH), (1, TOPK)),
                                 v(rsum, 0, (1, FH), (0, TOPK)), ALU.mult).then_inc(s_sel, 1)

            def second_part(n):
                dve.wait_ge(s_selc, n + 1)
                ve.scalar_tensor_tensor(w2_t[:, :], v(ps_s[0], 2 * TOK, (1, TOK), n=SEL), WSCALE, w1_t[:, :],
                                        ALU.mult, ALU.subtract).then_inc(s_w2, 1)

            def over_places(tensor, k, w):
                return v(tensor, k * CH, (2, CH // 2), (0, w), (1, 2), n=SEL)

            def all_places(tensor, w):
                return v(tensor, 0, (2 * w, CH // 2), (2, w), (1, 2), n=SEL)

            def places(w):
                return v(iota_e16, 0, (0, CH // 2), (2, w), (1, 2), n=SEL)

            def one_hots(n, k):
                if k == 0:
                    dve.wait_ge(s_w2, n + 1)
                if k >= 2:
                    dve.wait_ge(s_s, NCH * n + k - 1)
                need(dve, s_oh, NCH * n + k)
                cc.inc(ve.tensor_tensor(all_places(oh_e, ER), places(ER), over_places(lo_t, k, ER), ALU.is_equal))
                ve.tensor_tensor(all_places(oh_a[k % 2], P), places(P), over_places(hi_t, k, P), ALU.is_equal)

            def times_first_part(k):
                cc.wait()
                ve.tensor_tensor(all_places(oh_1[k % 2], ER), all_places(oh_e, ER), over_places(w1_t, k, ER), ALU.mult)

            def times_second_part(k):
                ve.tensor_tensor(all_places(oh_2[k % 2], ER), all_places(oh_e, ER), over_places(w2_t, k, ER),
                                 ALU.mult).then_inc(s_oh, 1)

            def weigh(n, k):
                if k == 0:
                    dve.wait_ge(s_gelu, 8 * n + 8)
                dve.wait_ge(s_s, NCH * n + k + 1)
                g = v(gh, k * CH, (TOK, ER), (1, CH))
                ve.tensor_tensor(g, g, v(ps_s[k % 2], 0, (1, ER), (ER, CH)), ALU.mult).then_inc(s_g, 1)

            def centre(n):
                dve.wait_ge(s_ymp, n + 1)
                ve.tensor_tensor(yc[:, :], yc[:, :], v(ps_f, 256, (1, W2)), ALU.subtract).then_inc(s_yc, 1)

            def normalize(n):
                dve.wait_ge(s_yrb, n + 1)
                ve.tensor_tensor(yc[:, :], yc[:, :], v(ps_f, 256, (1, W2)), ALU.mult).then_inc(s_yr, 1)

            def combine(n):
                dve.wait_ge(s_thf, n + 1)
                cf.link(ve.scalar_tensor_tensor(sg_f[:, :], sg_f[:, :], 1.0, v(ps_f, 0, (1, C)),
                                                ALU.add, ALU.mult))
                dve.wait_ge(s_oatt, n + 1)
                cf.link(ve.scalar_tensor_tensor(sg_f[:, :], sg_f[:, :], 0.5 / WSCALE, o_att[:, :],
                                                ALU.mult, ALU.mult))
                dve.wait_ge(s_xr, 16 * n + 16)
                ve.tensor_tensor(y_out[:, :], y_out[:, :], sg_f[:, :], ALU.add).then_inc(s_out, 1)

            def body(t, par, a, b, c, f):
                nxt = 1 - par
                ahead = not isinstance(t, int) or t + 2 < tiles
                for chain, on, n in ((ca, a, t + 1), (cb, b, t), (cc, c, t - 1), (cf, f, t - 2)):
                    if on:
                        chain.start(n)

                def beside(j):
                    if b and j - 1 in KEYS_AT:
                        next_places(key_rows(KEYS_AT.index(j - 1)))
                    if b and j - 1 in PAIRS_AT:
                        next_places(pair_rows(PAIRS_AT.index(j - 1)))
                    if c and j == 2:
                        second_part(t - 1)
                    if ahead and j == 30:
                        a_stats(t + 2)
                    if ahead and j == 31:
                        a_normalize(t + 2)
                    if f and j == 1:
                        combine(t - 2)
                    if a:
                        if j == 4:
                            a_shift(t + 1, nxt)
                        if j == 8:
                            dve.wait_ge(s_delta, t + 2)
                            for f_, m in ((0, 0), (0, 1), (1, 0), (1, 1), (2, 0), (2, 1)):
                                a_mixed(f_, m)
                        if j == 9:
                            a_mixed_add(t + 1, nxt)
                        if j == 20:
                            a_norm(t + 1)
                        if j == 21:
                            a_kmul(t + 1, nxt)
                            a_decay(t + 1)
                        if j == 23:
                            a_kfin(t + 1, nxt)
                            a_kk_b(t + 1, nxt)
                        if j == 25:
                            a_bonus(t + 1, nxt)
                    if b:
                        if j in KEYS_AT:
                            if j == KEYS_AT[0]:
                                dve.wait_ge(s_scores, 2 * t + 2)
                                dve.sem_inc(s_tick, 1)
                            first_eight(key_rows(KEYS_AT.index(j)))
                        if j == 9:
                            indices_as_floats()
                        if j == 10:
                            cb.wait()
                            pair_up(cand, topv, RUNS)
                            pair_up(candi, topif, RUNS[:3])
                        if j in PAIRS_AT:
                            cb.settle()
                            first_eight(pair_rows(PAIRS_AT.index(j)))
                        if j == 15:
                            differences()
                        if j in CODES_AT:
                            if j == CODES_AT[0] and a:
                                dve.wait_ge(s_scp, 2 * t + 3)
                            codes_match(2 * CODES_AT.index(j))
                        if j == 29:
                            coordinates(t)
                            softmax(t)
                    if c:
                        if j == 7:
                            centre(t - 1)
                        if j == 14:
                            normalize(t - 1)
                        if j in WEIGH_AT:
                            weigh(t - 1, WEIGH_AT.index(j))
                        if j in ONE_HOTS_AT:
                            one_hots(t - 1, ONE_HOTS_AT.index(j))

                def between(j):
                    if b and j in KEYS_AT:
                        strike_out(key_rows(KEYS_AT.index(j)))
                    if a and j == 8:
                        a_mixed(3, 0)
                    if b and j == 9:
                        high_parts()
                    if b and j == 10:
                        pair_up(candi, topif, RUNS[3:4])
                    if b and j in PAIRS_AT:
                        strike_out(pair_rows(PAIRS_AT.index(j)))
                    if c and j in ONE_HOTS_AT:
                        times_first_part(ONE_HOTS_AT.index(j))
                    if b and j in CODES_AT:
                        codes_pick(2 * CODES_AT.index(j))

                def after(j):
                    if b and j in KEYS_AT:
                        next_eight(key_rows(KEYS_AT.index(j)))
                    if a and j == 8:
                        a_mixed(3, 1)
                    if b and j == 9:
                        second_keys()
                    if b and j == 10:
                        cb.inc(pair_up(candi, topif, RUNS[4:]))
                    if b and j in PAIRS_AT:
                        next_eight(pair_rows(PAIRS_AT.index(j)))
                    if c and j in ONE_HOTS_AT:
                        times_second_part(ONE_HOTS_AT.index(j))
                    if b and j in CODES_AT:
                        codes_sum(2 * CODES_AT.index(j))

                for j in range(J):
                    if b:
                        of_step = lambda tensor: v(tensor[par], j, (TOK, HALVES), (J, B), (0, N))
                        if j == 0:
                            dve.wait_ge(s_kkb, t + 1)
                        need(dve, s_state, J * t + j)
                        ve.tensor_tensor(v(t_kk, 0, *STATE), state_after(j - 1), of_step(kk),
                                         ALU.mult).then_inc(s_tkk, 1)
                    beside(j)
                    if b:
                        dve.wait_ge(s_u, J * t + j + 1)
                        if j % 4 == 0:
                            need(dve, s_z, 8 * t + j // 4 - 1)
                        ve.tensor_tensor(state_after(j), v(ps_u, 0, *STATE), of_step(b_t), ALU.mult).then_inc(s_ub, 1)
                    between(j)
                    if b:
                        dve.wait_ge(s_ub, J * t + j + 1)
                        dve.wait_ge(s_dvk, J * t + j + 1)
                        ve.tensor_tensor(state_after(j), state_after(j), v(t_dvk, 0, *STATE),
                                         ALU.add).then_inc(s_state, 1)
                    after(j)
                for chain, on in ((ca, a), (cb, b), (cc, c), (cf, f)):
                    if on:
                        chain.end()

            a_stats(0)
            a_normalize(0)
            rounds(dve, body)

        @block.tensor
        def _(pe):
            te = nc.tensor

            def mm(o, lhs, rhs, first=True, last=True):
                return te.matmul(o, lhs, rhs, start=first, stop=last)

            ident = c_("ident", 0, (1, P))

            def a_transpose(n):
                pe.wait_ge(s_xn, n + 1)
                need(pe, s_scores, 2 * n)
                need(pe, s_da, DVE_LINKS[1] * n)
                for m in range(HALVES):
                    i = te.transpose(v(ps_a0, m * TOK, (1, TOK)), v(x_in, m * P, (1, P)), ident)
                i.then_inc(s_xtp, 1)

            def a_mix(n):
                pe.wait_ge(s_xxx, n + 1)
                for m in range(HALVES):
                    i = mm(v(ps_a1, 0, (1, TOK)), c_("w1", m * P, (1, P)), v(xxx, m * TOK, (1, TOK)), m == 0, m == 1)
                i.then_inc(s_mixp, 1)

            def a_delta(n):
                pe.wait_ge(s_mix, n + 1)
                for f in range(4):
                    for m in range(HALVES):
                        i = mm(v((ps_a0, ps_a1)[f // 2], (f % 2 * 2 + m) * TOK, (1, TOK)),
                               c_("w2", f * 256 + m * P, (1, P)), mix[:, :])
                i.then_inc(s_delta, 1)

            def project(o, off, name, f, m0, m, width):
                for h in range(HALVES):
                    i = mm(v(o, off, (1, TOK), n=m), c_(name, h * width + m0, (1, m)),
                           v(xf, (f * 2 + h) * TOK, (1, TOK)), h == 0, h == 1)
                return i

            def a_round1(n):
                pe.wait_ge(s_xf, n + 1)
                for m in range(HALVES):
                    project(ps_a0, m * TOK, "wr", 0, m * P, P, 256)
                for m in range(HALVES):
                    project(ps_a0, 256 + m * TOK, "wk", 2, m * P, P, 256)

            def a_round1_low(n):
                project(ps_a1, 0, "gw1", 0, 0, 128, 128)
                project(ps_a1, TOK, "lowa", 1, 0, 112, 112)
                project(ps_a1, 2 * TOK, "lowk", 2, 0, 112, 112).then_inc(s_p1, 1)

            def low_rank(o, off, name, src, row, rank):
                for m in range(HALVES):
                    i = mm(v(o, off + m * TOK, (1, TOK)), c_(name, m * P, (1, P), p0=row, n=rank),
                           v(src, 0, (1, TOK), p0=row, n=rank))
                return i

            def a_round2(n):
                pe.wait_ge(s_c1, n + 1)
                for m in range(HALVES):
                    project(ps_a0, m * TOK, "wv", 3, m * P, P, 256)
                low_rank(ps_a1, 0, "low2", low_a, 0, 64)
                low_rank(ps_a1, 256, "low2", low_a, 64, 16).then_inc(s_p2, 1)

            def a_round3(n):
                pe.wait_ge(s_c2, n + 1)
                pe.wait_ge(s_vt, n + 1)
                low_rank(ps_a0, 0, "low2", low_a, 96, 16)
                low_rank(ps_a0, 256, "lowk2", low_k, 96, 16)
                low_rank(ps_a1, 0, "lowk2", low_k, 0, 16)
                for m in range(HALVES):
                    i = mm(v(ps_a1, 256 + m * TOK, (1, TOK)), c_("gw2", m * P, (1, P)), tgate[:, :])
                i.then_inc(s_p3, 1)

            def head_sums(o, src, done):
                for m in range(HALVES):
                    i = mm(v(o, m * HH, (1, HH)), v(src, m * TOK, (1, TOK)), c_("headcol", 0, (1, HH)))
                i.then_inc(done, 1)

            def over_channels(o, src, done):
                for m in range(HALVES):
                    i = mm(o(m * TOK), c_("headrow", m * P, (1, P), n=H), v(src, 0, (1, TOK), n=H))
                i.then_inc(done, 1)

            def a_bonus(n):
                pe.wait_ge(s_rkf, n + 1)
                pe.wait_ge(s_kkb, n + 1)
                mm(v(ps_a1, 0, (1, W2)), c_("headones", 0, (1, P)), rkf[:, :]).then_inc(s_bonus, 1)

            def a_queries(n, p, m0):
                if m0 == 0:
                    pe.wait_ge(s_c3, n + 1)
                for m in range(m0, m0 + 2):
                    for h in range(HALVES):
                        i = mm(v(ps_a0, m * TOK, (1, TOK)), c_("wq", h * 512 + m * P, (1, P)),
                               v(xnt[p], h * TOK, (1, TOK)), h == 0, h == 1)
                if m0 == 2:
                    i.then_inc(s_q, 1)

            def a_scores(n, i):
                if i == 0:
                    pe.wait_ge(s_qt, n + 1)
                else:
                    pe.wait_ge(s_scores, 2 * n + 1)
                for m in (0, 1):
                    last = mm(v(ps_a0, m * 256, (1, 256)), v(q_t, (2 * i + m) * TOK, (1, TOK)), c_("kbd", 0, (1, 256)))
                last.then_inc(s_scp, 1)

            def b_picks(n):
                pe.wait_ge(s_sel, n + 1)
                need(pe, s_g, NCH * n)
                for m, src in enumerate((hif, lof, wsel)):
                    i = te.transpose(v(ps_s[0], m * TOK, (1, TOK), n=SEL), src[:, :], ident)
                i.then_inc(s_selp, 1)

            def c_down(n, u):
                q = u // 2
                if u == 0:
                    pe.wait_ge(s_xh, n + 1)
                if u % 2 == 0 and (q >= 2 or not isinstance(n, int) or n > 0):
                    pe.wait_ge(s_gelu, 8 * n + q - 1)
                for e in (2 * u, 2 * u + 1):
                    for h in range(HALVES):
                        i = mm(v(ps_h[q % 2], e % 4 * TOK, (1, TOK)), v(wdown, (h * ER + e) * P, (1, P)),
                               v(xh, h * TOK, (1, TOK)), h == 0, h == 1)
                if u % 2 == 1:
                    i.then_inc(s_h, 1)

            def c_weights(n, k):
                pe.wait_ge(s_oh, NCH * n + k + 1)
                if k >= 2:
                    pe.wait_ge(s_g, NCH * n + k - 1)
                for m in range(CH):
                    o = v(ps_s[k % 2], m * ER, (1, ER))
                    lhs = v(oh_a[k % 2], (m // 2) * 2 * P + m % 2, (2, P), n=SEL)
                    at = (m // 2) * 2 * ER + m % 2
                    mm(o, lhs, v(oh_1[k % 2], at, (2, ER), n=SEL), True, False)
                    i = mm(o, lhs, v(oh_2[k % 2], at, (2, ER), n=SEL), False, True)
                i.then_inc(s_s, 1)

            def c_y(n, v0, v1):
                if v0 == 0:
                    pe.wait_ge(s_z, 8 * n + 8)
                    need(pe, s_out, n)
                for m in range(v0, v1):
                    i = mm(v(ps_f, m // N * TOK, (1, TOK)), c_("spread", N - 1 - m % N, (1, P)),
                           v(zr, m * TOK, (1, TOK)), m % N == 0, m % N == N - 1)
                if v1 == 2 * N:
                    i.then_inc(s_y, 1)

            def c_means(n):
                pe.wait_ge(s_ys, n + 1)
                mm(v(ps_f, 256, (1, W2)), c_("headmean", 0, (1, P)), yc[:, :]).then_inc(s_ymp, 1)

            def c_project(n):
                pe.wait_ge(s_yn, n + 1)
                for m in range(HALVES):
                    i = mm(v(ps_f, 256, (1, C)), v(yc, m * TOK, (1, TOK)), c_("wo", m * 256, (1, 256)), m == 0, m == 1)
                i.then_inc(s_o, 1)

            def c_up(n, e0, e1):
                if e0 == 0:
                    pe.wait_ge(s_g, NCH * n + NCH)
                    pe.wait_ge(s_oatt, n + 1)
                for e in range(e0, e1):
                    i = mm(v(ps_f, 0, (1, C)), v(gh, e * TOK, (1, TOK)), v(wup, e * C, (1, C)), e == 0, e == ER - 1)
                if e1 == ER:
                    i.then_inc(s_up, 1)

            def body(t, par, a, b, c, f):
                nxt = 1 - par
                n = t + 1
                for j in range(J):
                    if b:
                        pe.wait_ge(s_tkk, J * t + j + 1)
                        mm(v(ps_u, 0, (1, SW)), c_("headones", 0, (1, P)), t_kk[:, :]).then_inc(s_u, 1)

                    if c:
                        if j == 6:
                            c_means(t - 1)
                        if j == 8:
                            pe.wait_ge(s_ysq, t)
                            head_sums(ps_f, ysq, s_yvp)
                        if j == 12:
                            pe.wait_ge(s_yrs, 3 * t)
                            te.transpose(v(ps_f, 0, (1, TOK), n=H), yrs[:, :], ident).then_inc(s_yrtp, 1)
                        if j == 13:
                            pe.wait_ge(s_yrt, t)
                            over_channels(lambda at: v(ps_f, 256 + at, (1, TOK)), yrs_t, s_yrb)
                        if j == 16:
                            c_project(t - 1)
                        if j in WEIGHTS_AT:
                            c_weights(t - 1, WEIGHTS_AT.index(j))
                    if a:
                        if j == 2:
                            a_transpose(n)
                        if j == 5:
                            a_mix(n)
                        if j == 6:
                            a_delta(n)
                        if j == 10:
                            a_round1(n)
                        if j == 11:
                            a_round1_low(n)
                        if j == 14:
                            a_round2(n)
                        if j == 17:
                            a_round3(n)
                        if j == 19:
                            pe.wait_ge(s_sq, n + 1)
                            head_sums(ps_a1, kk_sq, s_ssp)
                        if j in (19, 20):
                            a_queries(n, nxt, 2 * (j - 19))
                        if j == 21:
                            pe.wait_ge(s_inv, n + 1)
                            te.transpose(v(ps_a1, TOK, (1, TOK), n=H), inv_n[:, :], ident).then_inc(s_invtp, 1)
                        if j == 22:
                            pe.wait_ge(s_invt, n + 1)
                            over_channels(lambda at: v(ps_a1, 256 + at, (1, TOK)), inv_t, s_invb)
                            a_scores(n, 0)
                        if j == 24:
                            a_bonus(n)
                        if j == 23:
                            a_scores(n, 1)
                    if c:
                        if j in Y_AT:
                            c_y(t - 1, 8 * Y_AT.index(j), 8 * Y_AT.index(j) + 8)
                        for u, at in enumerate(DOWN_AT):
                            if j == at:
                                c_down(t - 1, u)
                        if j >= UP_AT:
                            c_up(t - 1, UP_ROWS[j - UP_AT], UP_ROWS[j - UP_AT + 1])
                if b:
                    b_picks(t)

            pe.wait_ge(s_par, 64)
            rounds(pe, body)


def pack(inputs):
    import numpy as np
    g = {k: np.asarray(a) for k, a in inputs.items()}
    p = "L0_attn_"
    z = np.zeros((P, NCONST), g[p + "x"].dtype)

    def put(name, a, r0=0, off=0):
        a = np.asarray(a)
        z[r0:r0 + a.shape[0], COL[name] + off:COL[name] + off + a.shape[1]] = a

    def halves(name, wt):
        for c in range(2):
            put(name, wt[c * P:(c + 1) * P], off=c * wt.shape[1])

    halves("w1", g[p + "time_maa_w1"].T)
    for f in range(4):
        put("w2", g[p + "time_maa_w2"][f].T, r0=32 * f, off=256 * f)
    halves("wr", g[p + "receptance"].T)
    halves("wk", g[p + "key_w"].T)
    halves("wv", g[p + "value"].T)
    halves("gw1", g[p + "gate_w1"].T)
    pad = np.zeros((16, C), z.dtype)
    halves("lowa", np.concatenate([g[p + "time_decay_w1"], g[p + "time_aaa_w1"], pad, g[p + "ma_w1"]], 0).T)
    halves("lowk", np.concatenate([g[p + "time_kkk_w1"], *5 * [pad], g[p + "mk_w1"]], 0).T)
    for name, row in (("time_decay_w2", 0), ("time_aaa_w2", 64), ("ma_w2", 96)):
        put("low2", g[p + name].T, row)
    put("lowk2", g[p + "time_kkk_w2"].T, 0)
    put("lowk2", g[p + "mk_w2"].T, 96)
    put("gw2", g[p + "gate_w2"].T)
    halves("wq", g["L0_ffn_Wq"])
    for a in range(2):
        put("kbd", g["L0_ffn_K1"].T, 64 * a, 128 * a)
        put("kbd", g["L0_ffn_K2"].T, 64 * a + 32, 128 * a + 64)
    halves("wo", g[p + "output"].T)
    put("ident", np.eye(P))
    put("headones", np.kron(np.eye(HH), np.ones((N, N))))
    put("headcol", np.kron(np.eye(HH), np.ones((N, 1))))
    for c in range(2):
        put("headrow", np.kron(np.eye(HH), np.ones((1, N))), 8 * c, P * c)
    put("headmean", np.kron(np.eye(HH), np.full((N, N), 1 / N)))
    put("spread", np.kron(np.eye(HH), np.ones((N, 1)) * (np.arange(N) == 0)), off=N - 1)
    cols = lambda a: np.asarray(a).reshape(-1, P).T
    put("maax", cols(g[p + "time_maa_x"]))
    put("maa", cols(g[p + "time_maa"]))
    put("td", cols(g[p + "time_decay"]))
    put("ba", cols(g[p + "time_aaaaa"]))
    put("bma", cols(g[p + "time_misc_a"]))
    put("bmk", cols(g[p + "time_misc_k"]))
    put("fa", cols(g[p + "time_faaaa"]))
    put("bq", cols(g["L0_ffn_bq"]))
    put("lnw", cols(g[p + "ln_w"]))
    put("lnb", cols(g[p + "ln_b"]))
    put("iota_c", np.broadcast_to(np.arange(NCAND), (P, NCAND)))
    put("mhalf", np.full((P, H), -0.5))
    def experts(w):
        return w[:NKEY * NKEY].reshape(NKEY, 2, ER, C).transpose(1, 0, 2, 3)
    up = np.ascontiguousarray(experts(g["L0_ffn_W_up"]).reshape(P, ER * C))
    down = experts(g["L0_ffn_W_down"]).reshape(P, ER, 2, P).transpose(3, 2, 1, 0)
    iota_e = np.broadcast_to(np.repeat(np.arange(P), 2), (P, 2 * P)).astype(z.dtype)
    return z, np.ascontiguousarray(down.reshape(P, 2 * ER * P)), up, iota_e


def kernel(**inputs):
    import numpy as _np
    import concourse.bacc as _bacc
    from concourse.bass_utils import run_bass_kernel_spmd as _run

    x = _np.asarray(inputs["L0_attn_x"])
    tiles = x.shape[1] // J
    xt = _np.ascontiguousarray(x.reshape(B, tiles, J, C).transpose(1, 0, 2, 3).reshape(tiles * TOK, C))
    params, down, up, iota_e = pack(inputs)
    arrays = {"in_x": xt, "in_params": params, "in_down": down, "in_up": up, "in_iota": iota_e}
    nc = _bacc.Bacc("TRN2", target_bir_lowering=False, num_devices=1)
    aps = [nc.dram_tensor(n, a.shape, F32, kind="ExternalInput").ap() for n, a in arrays.items()]
    vs = nc.dram_tensor("v_scratch", (C, TOK), F32, kind="Internal").ap()
    out = nc.dram_tensor("out_0", (tiles * TOK, C), F32, kind="ExternalOutput").ap()
    build(nc, *aps, vs, out, tiles)
    r = _run(nc, [arrays], core_ids=[0])
    y = _np.asarray(r.results[0]["out_0"])
    return y.reshape(tiles, B, J, C).transpose(1, 0, 2, 3).reshape(x.shape)
```
